# Optimizing a Trainium2 kernel written in Bass

```python
import numpy as np
import jax
import jax.numpy as jnp

def _softmax(x, axis=-1):
    return jax.nn.softmax(x, axis=axis)

def _gelu(x):
    return jax.nn.gelu(x, approximate=True)

def _silu(x):
    return jax.nn.silu(x)

def _sigmoid(x):
    return jax.nn.sigmoid(x)

def _layernorm(x, axis=-1, eps=1e-05):
    m = jnp.mean(x, axis=axis, keepdims=True)
    v = jnp.var(x, axis=axis, keepdims=True)
    return (x - m) / jnp.sqrt(v + eps)

def _scatter_add(tgt, idx, src, axis=0):
    return tgt.at[idx].add(src)

def _segment_sum(src, seg, n):
    return jax.ops.segment_sum(src, seg, n)
kernel_name = 'mk_gps_d1_gnn_r32_0899ed'

def setup_inputs(seed: int=0):
    np.random.seed(seed)
    _w = jnp.asarray

    def _rec_inputs():
        import jax
        import jax.numpy as jnp
        _gk = jax.random.key(seed)
        x = -8.776e-05 + 1 * jax.random.normal(jax.random.fold_in(_gk, 1), (625, 256), jnp.float32)
        src = jax.random.randint(jax.random.fold_in(_gk, 2), (20000,), 0, 625, jnp.int32)
        dst = jax.random.randint(jax.random.fold_in(_gk, 3), (20000,), 0, 625, jnp.int32)
        _o = jnp.argsort(dst, stable=True)
        src = src[_o]
        dst = dst[_o]
        return (x, src, dst)
    x, src, dst = _rec_inputs()

    def _L0_gnn_setup():
        import jax, jax.numpy as jnp
        import numpy as np
        N_NODES = 625
        key = jax.random.key(seed)
        k1, k2, k3, k4 = jax.random.split(key, 4)
        d = 256
        E = 10000
        x = jax.random.normal(k1, (N_NODES, d), dtype=jnp.float32)
        edge_index = jax.random.randint(k2, (2, E), 0, N_NODES, dtype=jnp.int64)
        limit = float(np.sqrt(6.0 / (d + d)))
        W_l = jax.random.uniform(k3, (d, d), dtype=jnp.float32, minval=-limit, maxval=limit)
        W_r = jax.random.uniform(k4, (d, d), dtype=jnp.float32, minval=-limit, maxval=limit)
        b_r = jnp.zeros((d,), dtype=jnp.float32)
        return {'x': x, 'edge_index': edge_index, 'W_l': W_l, 'W_r': W_r, 'b_r': b_r}
    _L0_gnn_all = _L0_gnn_setup()
    _L0_gnn_in = {k: v for k, v in _L0_gnn_all.items() if k in ('W_l', 'W_r', 'b_r')}
    del _L0_gnn_all

    def _L0_mix_setup():
        import jax, jax.numpy as jnp
        import numpy as np
        A, Bc, Cc = (0.5, 1.0, 1.0)
        H = 8
        EPS = 1e-12

        def _normalize(t):
            n = jnp.linalg.norm(t, axis=-1, keepdims=True)
            return t / jnp.maximum(n, EPS)
        key = jax.random.key(seed)
        ks = jax.random.split(key, 5)
        B, N, C = (8, 64, 256)
        D = C // H
        x = jax.random.normal(ks[0], (B, N, C), dtype=jnp.float32)
        Wqkv = jax.random.normal(ks[1], (3 * H * D, C), dtype=jnp.float32) * 0.02
        bqkv = jnp.zeros((3 * H * D,), dtype=jnp.float32)
        Wproj = jax.random.normal(ks[2], (C, H * D), dtype=jnp.float32) * 0.02
        bproj = jnp.zeros((C,), dtype=jnp.float32)
        temperature = jnp.ones((1, H, 1, 1), dtype=jnp.float32)
        return {'x': x, 'Wqkv': Wqkv, 'bqkv': bqkv, 'Wproj': Wproj, 'bproj': bproj, 'temperature': temperature}
    _L0_mix_all = _L0_mix_setup()
    _L0_mix_in = {k: v for k, v in _L0_mix_all.items() if k in ('Wqkv', 'bqkv', 'Wproj', 'bproj', 'temperature')}
    del _L0_mix_all

    def _L0_ffn_setup():
        import jax, jax.numpy as jnp
        import numpy as np
        C = 256
        HID = 1024
        E = 8
        TEMP = 1.0
        key = jax.random.key(seed)
        ks = jax.random.split(key, 7)
        x = jax.random.normal(ks[0], (8, 512, C), dtype=jnp.float32)
        W1 = jax.random.normal(ks[1], (C, HID), dtype=jnp.float32) * 0.02
        b1 = jnp.zeros((HID,), dtype=jnp.float32)
        Wg = jax.random.normal(ks[2], (HID, E), dtype=jnp.float32) * 0.02
        bg = jnp.zeros((E,), dtype=jnp.float32)
        Wd = jax.random.normal(ks[3], (E, HID, C), dtype=jnp.float32) * 0.02
        bd = jnp.zeros((E, C), dtype=jnp.float32)
        return {'x': x, 'W1': W1, 'b1': b1, 'Wg': Wg, 'bg': bg, 'Wd': Wd, 'bd': bd}
    _L0_ffn_all = _L0_ffn_setup()
    _L0_ffn_in = {k: v for k, v in _L0_ffn_all.items() if k in ('W1', 'b1', 'Wg', 'bg', 'Wd', 'bd')}
    del _L0_ffn_all
    return {'x': x, 'src': src, 'dst': dst, 'L0_gnn_W_l': _L0_gnn_in['W_l'], 'L0_gnn_W_r': _L0_gnn_in['W_r'], 'L0_gnn_b_r': _L0_gnn_in['b_r'], 'L0_mix_Wqkv': _L0_mix_in['Wqkv'], 'L0_mix_bqkv': _L0_mix_in['bqkv'], 'L0_mix_Wproj': _L0_mix_in['Wproj'], 'L0_mix_bproj': _L0_mix_in['bproj'], 'L0_mix_temperature': _L0_mix_in['temperature'], 'L0_ffn_W1': _L0_ffn_in['W1'], 'L0_ffn_b1': _L0_ffn_in['b1'], 'L0_ffn_Wg': _L0_ffn_in['Wg'], 'L0_ffn_bg': _L0_ffn_in['bg'], 'L0_ffn_Wd': _L0_ffn_in['Wd'], 'L0_ffn_bd': _L0_ffn_in['bd']}

def reference(x, src, dst, L0_gnn_W_l, L0_gnn_W_r, L0_gnn_b_r, L0_mix_Wqkv, L0_mix_bqkv, L0_mix_Wproj, L0_mix_bproj, L0_mix_temperature, L0_ffn_W1, L0_ffn_b1, L0_ffn_Wg, L0_ffn_bg, L0_ffn_Wd, L0_ffn_bd):
    import jax
    import jax.numpy as jnp

    def _L0_gnn_ref(x, edge_index, W_l, W_r, b_r):
        import jax, jax.numpy as jnp
        import numpy as np
        N_NODES = 625
        src, dst = (edge_index[0], edge_index[1])
        messages = x[src]
        sums = jax.ops.segment_sum(messages, dst, num_segments=N_NODES)
        counts = jax.ops.segment_sum(jnp.ones_like(dst, dtype=x.dtype), dst, num_segments=N_NODES)
        aggr = sums / jnp.maximum(counts, 1.0)[:, None]
        out = aggr @ W_l.T + x @ W_r.T + b_r
        return out

    def _L0_mix_ref(x, Wqkv, bqkv, Wproj, bproj, temperature):
        import jax, jax.numpy as jnp
        import numpy as np
        A, Bc, Cc = (0.5, 1.0, 1.0)
        H = 8
        EPS = 1e-12

        def _normalize(t):
            n = jnp.linalg.norm(t, axis=-1, keepdims=True)
            return t / jnp.maximum(n, EPS)
        B, N, C = x.shape
        D = C // H
        scale = float(D) ** 0.25
        qkv = (x @ Wqkv.T + bqkv).reshape(B, N, 3, H, D)
        qkv = jnp.transpose(qkv, (2, 0, 3, 1, 4))
        q, k, v = (qkv[0], qkv[1], qkv[2])
        q = q * scale
        v1 = jnp.concatenate([jnp.ones((B, H, N, 1), dtype=v.dtype), v], axis=-1)
        qn = _normalize(q) * (scale * temperature)
        kn = _normalize(k) * scale
        vN = v1 / N
        kv_mod = jnp.einsum('bhni,bhnj,bhne->bhije', kn, kn, vN)
        kv = jnp.einsum('bhnd,bhne->bhde', kn, vN)
        vsum = jnp.sum(vN, axis=-2)[:, :, None, :]
        y = A * jnp.einsum('bhni,bhnj,bhije->bhne', qn, qn, kv_mod) + scale ** 2 * Bc * jnp.einsum('bhnd,bhde->bhne', qn, kv) + scale ** 4 * Cc * vsum
        y_norm, y = (y[..., :1], y[..., 1:])
        y = y / y_norm
        out = jnp.transpose(y, (0, 2, 1, 3)).reshape(B, N, H * D)
        return out @ Wproj.T + bproj

    def _L0_ffn_ref(x, W1, b1, Wg, bg, Wd, bd):
        import jax, jax.numpy as jnp
        import numpy as np
        C = 256
        HID = 1024
        E = 8
        TEMP = 1.0
        orig_shape = x.shape
        xf = x.reshape(-1, orig_shape[-1])
        H = jax.nn.gelu(xf @ W1 + b1, approximate=False)
        probs = jax.nn.softmax((H @ Wg + bg) / TEMP, axis=-1)
        assign = jnp.argmax(probs, axis=-1)
        out = jnp.zeros_like(xf)
        for e in range(Wd.shape[0]):
            y = H @ Wd[e] + bd[e]
            sel = (assign == e)[:, None]
            out = out + jnp.where(sel, probs[:, e:e + 1] * y, 0.0)
        return out.reshape(orig_shape)
    edge_index = jnp.stack([src, dst])
    xn = _layernorm(x, axis=-1)
    x = x + _L0_gnn_ref(xn, edge_index, L0_gnn_W_l, L0_gnn_W_r, L0_gnn_b_r) + _L0_mix_ref(xn[None], L0_mix_Wqkv, L0_mix_bqkv, L0_mix_Wproj, L0_mix_bproj, L0_mix_temperature)[0]
    x = x + _L0_ffn_ref(_layernorm(x, axis=-1)[None], L0_ffn_W1, L0_ffn_b1, L0_ffn_Wg, L0_ffn_bg, L0_ffn_Wd, L0_ffn_bd)[0]
    return x

_drawn_inputs = setup_inputs


def setup_inputs(seed=0):
    import zlib

    import numpy as np

    out = dict(_drawn_inputs(seed))
    spreads = {'L0_gnn_b_r': (0.0, 0.1),
     'L0_mix_bqkv': (0.0, 0.384),
     'L0_mix_bproj': (0.0, 0.1),
     'L0_mix_temperature': (1.0, 0.6),
     'L0_ffn_b1': (0.0, 0.793),
     'L0_ffn_bg': (0.0, 0.542),
     'L0_ffn_bd': (0.0, 0.8)}
    factors = {'L0_mix_Wqkv': 8.0,
     'L0_mix_Wproj': 2.706,
     'L0_ffn_W1': 3.789,
     'L0_ffn_Wg': 4.095,
     'L0_ffn_Wd': 4.634}
    for name, (base, spread) in spreads.items():
        noise = np.random.default_rng([zlib.crc32(name.encode()), seed]).standard_normal(out[name].shape)
        drawn = base * np.exp(spread * noise) if base else spread * noise
        out[name] = jnp.asarray(drawn.astype(out[name].dtype))
    for name, factor in factors.items():
        out[name] = (out[name] * factor).astype(out[name].dtype)
    return out
```

```python
from contextlib import ExitStack

import concourse.bass as bass
from concourse import mybir

F32 = mybir.dt.float32
F16 = mybir.dt.float16
BF16 = mybir.dt.bfloat16
I32 = mybir.dt.int32
ALU = mybir.AluOpType
ACT = mybir.ActivationFunctionType
AX = mybir.AxisListType

P = 128
LN_EPS = 1e-5
NORM_EPS = 1e-12


def gps_layer(nc, x, src, dst, w_qkv, b_qkv, w_lr, b_r, w_proj, b_proj, temp,
              w1, b1, wg, bg, wd, bd, out):
    N, C = x.shape
    TP = 125
    T = N // TP
    KC = C // P
    NCH = src.shape[1]
    GC = 8
    NG = NCH // GC
    OHW = TP * (T - 1) + P
    H = temp.shape[1]
    D = C // H
    HG = P // D
    SC2 = float(D) ** 0.5
    SC = SC2 ** 0.5
    HID = w1.shape[2]
    KH = HID // P
    E = bg.shape[1]
    HALF = [(0, (N + 1) // 2), ((N + 1) // 2, N)]
    HW = HALF[0][1]
    BANK = 512
    SPLIT = [(0, BANK), (BANK, N)]
    assert N == T * TP and NG * GC == NCH and NG % 2 == 0 and H == 2 * HG

    with ExitStack() as ctx:
        def sb(name, shape, dt=F32):
            return ctx.enter_context(nc.sbuf_tensor(name, shape, dt))

        def sem(name):
            return ctx.enter_context(nc.semaphore(name))

        ps = ctx.enter_context(nc.psum_tensor("ps", [P, 8, BANK], F32))
        psf = ps[:, :, :].rearrange("p b n -> p (b n)")

        x_sb = sb("x_sb", [TP, T, C])
        src_i = sb("src_i", [TP, NCH], I32)
        dst_i = sb("dst_i", [TP, NCH], I32)
        wqkv_sb = sb("wqkv_sb", [P, KC, 3 * C])
        bqkv_sb = sb("bqkv_sb", [1, 3 * C])
        wlr_sb = sb("wlr_sb", [P, KC, 2 * C])
        wproj_sb = sb("wproj_sb", [P, KC, C])
        br_sb = sb("br_sb", [TP, C])
        bproj_sb = sb("bproj_sb", [TP, C])
        temp_sb = sb("temp_sb", [TP, H])
        w1_sb = sb("w1_sb", [P, KC, HID])
        b1_sb = sb("b1_sb", [P, KH])
        wg_sb = sb("wg_sb", [P, KH, E])
        bg_sb = sb("bg_sb", [TP, E])
        wd_sb = sb("wd_sb", [P, E, KH, C])
        bd_sb = sb("bd_sb", [E, C])
        ident = sb("ident", [P, P])
        blk = sb("blk", [P, P])
        node_ids = sb("node_ids", [TP, OHW], F16)
        ones_c = sb("ones_c", [P, P])
        sc2_col = sb("sc2_col", [P, 1])
        zeros = sb("zeros", [TP, BANK], BF16)
        thr = sb("thr", [TP, T + 1])
        bits = sb("bits", [1, T])
        erank = sb("erank", [TP, E])
        src_f = sb("src_f", [TP, NCH])
        dst_f = sb("dst_f", [TP, NCH])
        in_tile = sb("in_tile", [TP, T, NG])
        flag_f = sb("flag_f", [1, T, NG])
        flag_g = sb("flag_g", [1, NG])
        flags = sb("flags", [1, NG], I32)
        big = sb("big", [P, 2 * 2 * GC * OHW // 2])
        at_sb = sb("at_sb", [P, T * N])
        qk_sb = sb("qk_sb", [P, 2560])
        oh = big[0:TP, :].bitcast(BF16).rearrange("p (b w j n) -> p b w j n", b=2, w=2, j=GC)
        ge = big[0:TP, 0:(T + 1) * NCH].rearrange("p (k n) -> p k n", k=T + 1)
        inr = big[0:TP, (T + 1) * NCH:(2 * T + 1) * NCH].rearrange("p (k n) -> p k n", k=T)
        hT = big[:, 0:KH * N].rearrange("p (k n) -> p k n", k=KH)
        qkT = big[:, KH * N:(KH + 4) * N].rearrange("p (k n) -> p k n", k=4)
        rn = big[:, (KH + 4) * N:(KH + 6) * N].rearrange("p (k n) -> p k n", k=2)
        bn = sb("bn", [TP, T, 6])
        mv = sb("mv", [TP, T, 2])
        rstd = sb("rstd", [TP, T])
        xn = sb("xn", [TP, T, C])
        xnT = sb("xnT", [P, KC, N])
        xb = sb("xb", [TP, T, C])
        qk = qk_sb[0:TP, :].rearrange("p (t c) -> p t c", t=T)
        sq = at_sb[0:TP, 0:T * 2 * C].rearrange("p (t c) -> p t c", t=T)
        v = sb("v", [TP, T, C])
        z = sb("z", [TP, T, C + 1])
        nrm = sb("nrm", [TP, 2, T, H])
        MA = sb("MA", [P, 2, P])
        ks = sb("ks", [P, 2])
        vs = sb("vs", [P, 2])
        NGB = 4
        g = qk_sb[0:TP, 0:NGB * 2 * HW].rearrange("p (b i n) -> p b i n", b=NGB, i=2)
        yT = sb("yT", [P, 2, N])
        uq = yT
        AT = at_sb[0:TP, :].rearrange("p (s n) -> p s n", s=T)
        cnt = sb("cnt", [TP, T])
        x2 = sb("x2", [TP, T, C])
        x2n = xn
        x2nT = xnT
        lg = sb("lg", [TP, T, E])
        mx = sb("mx", [TP, T])
        ex = sb("ex", [TP, T, E])
        se = sb("se", [TP, T])
        eq = sb("eq", [TP, T, E])
        rk = sb("rk", [TP, T])
        selp = sb("selp", [TP, T, E])
        selT = sb("selT", [E, N])

        (in_e, in_x, in_wqkv, in_bqkv, in_wlr, in_bias, in_wproj, in_w1, in_gate, in_wd, in_bd) = (
            sem(n) for n in ("in_edges", "in_x", "in_wqkv", "in_bqkv", "in_wlr", "in_bias", "in_wproj",
                             "in_w1", "in_gate", "in_wd", "in_bd"))
        pool_const = sem("pool_const")
        pool_chain = sem("pool_chain")
        dve_chain = sem("dve_chain")
        (flag_rows, flag_sum, flags_ready, oh_ready, oh_free, var_ready, std_ready, xn_ready, xT_ps,
         xT_ready, qkv_ps, qkv_copied, norm_sq, norm_sd, qk_scaled, qkT_ps, qkT_copied, A_done, A_copied,
         xb_ready, m_ps, m_ready, u_ps, u_ready, n_ps, n_ready, s_ps, g_ready, g_used, y_ready,
         rp_ps, x2_ready, f_ps, h_ready, lg_ps, ex_in, ex_ready, sel_ready, selT_ps, selT_ready, bd_ps,
         acc_ready, e_ps, out_sent) = (
            sem(n) for n in ("flag_rows", "flag_sum", "flags_ready", "oh_ready", "oh_free", "var_ready",
                             "std_ready", "xn_ready", "xT_ps", "xT_ready", "qkv_ps", "qkv_copied", "norm_sq",
                             "norm_sd", "qk_scaled", "qkT_ps", "qkT_copied", "A_done", "A_copied", "xb_ready",
                             "m_ps", "m_ready", "u_ps", "u_ready", "n_ps", "n_ready", "s_ps", "g_ready",
                             "g_used", "y_ready", "rp_ps", "x2_ready", "f_ps", "h_ready", "lg_ps",
                             "ex_in", "ex_ready", "sel_ready", "selT_ps", "selT_ready", "bd_ps", "acc_ready",
                             "e_ps", "out_sent"))

        def a_block(s, t):
            return ps[:, s, TP * t:TP * (t + 1)] if t < 4 else ps[:, 5 + s // 4, TP * (s % 4):TP * (s % 4 + 1)]

        def wide(b):
            return psf[:, BANK * b:BANK * b + T * P].rearrange("p (t n) -> p t n", n=P)[:, :, 0:TP]

        def tiles(row):
            return row.rearrange("p (t n) -> p t n", n=TP)

        units = [(hg, hf, m, pr) for hg in range(2) for hf in range(2) for m in range(T) for pr in range(2)]
        SLOTS = 3

        block = ctx.enter_context(nc.Block())

        @block.sync
        def _(sp):
            sp.dma_start(src_i[:, :], src).then_inc(in_e, 16)
            sp.dma_start(dst_i[:, :], dst).then_inc(in_e, 16)
            sp.dma_start(wqkv_sb[:, :, :], w_qkv).then_inc(in_wqkv, 16)
            sp.dma_start(bqkv_sb[:, :], b_qkv).then_inc(in_bqkv, 16)
            sp.dma_start(wlr_sb[:, :, :], w_lr).then_inc(in_wlr, 16)
            sp.dma_start(br_sb[:, :], b_r.partition_broadcast(TP)).then_inc(in_bias, 16)
            sp.dma_start(bproj_sb[:, :], b_proj.partition_broadcast(TP)).then_inc(in_bias, 16)
            sp.dma_start(temp_sb[:, :], temp.partition_broadcast(TP)).then_inc(in_bias, 16)
            sp.dma_start(wproj_sb[:, :, :], w_proj).then_inc(in_wproj, 16)
            sp.dma_start(w1_sb[:, :, :], w1).then_inc(in_w1, 16)
            sp.dma_start(b1_sb[:, :], b1).then_inc(in_gate, 16)
            sp.dma_start(wg_sb[:, :, :], wg).then_inc(in_gate, 16)
            sp.dma_start(bg_sb[:, :], bg.partition_broadcast(TP)).then_inc(in_gate, 16)
            sp.dma_start(bd_sb[:, :], bd).then_inc(in_bd, 16)
            for e in range(E):
                sp.dma_start(wd_sb[:, e, :, :], wd[:, e, :, :]).then_inc(in_wd, 16)
            for t in range(T):
                sp.wait_ge(acc_ready, T * E + t + 1)
                sp.dma_start(out[TP * t:TP * (t + 1), :], x2[:, t, :]).then_inc(out_sent, 16)
            sp.wait_ge(out_sent, 16 * T)

        @block.gpsimd
        def _(pool):
            made = [0]

            def step(ins):
                made[0] += 1
                ins.then_inc(pool_chain, 1)
                pool.wait_ge(pool_chain, made[0])

            step(nc.gpsimd.iota(node_ids[:, :], pattern=[[1, OHW]], base=0, channel_multiplier=0,
                                allow_small_or_imprecise_dtypes=True))
            step(nc.gpsimd.iota(thr[:, :], pattern=[[TP, T + 1]], base=0, channel_multiplier=0,
                                allow_small_or_imprecise_dtypes=True))
            for t in range(T):
                step(nc.gpsimd.memset(bits[:, t:t + 1], float(2 ** t)))
            step(nc.gpsimd.memset(ones_c[:, :], 1.0))
            step(nc.gpsimd.memset(ident[:, :], 0.0))
            step(nc.gpsimd.affine_select(out=ident[:, :], in_=ident[:, :], compare_op=ALU.not_equal, fill=1.0,
                                         base=0, pattern=[[-1, P]], channel_multiplier=1))
            nc.gpsimd.memset(zeros[:, :], 0.0).then_inc(pool_const, 1)
            step(nc.gpsimd.iota(erank[:, :], pattern=[[-1, E]], base=E, channel_multiplier=0,
                                allow_small_or_imprecise_dtypes=True))
            b4 = blk[:, :].rearrange("p (j d) -> p j d", d=D)
            step(nc.gpsimd.memset(blk[:, :], 1.0))
            step(nc.gpsimd.affine_select(out=b4, in_=b4, compare_op=ALU.is_ge, fill=0.0,
                                         base=0, pattern=[[-D, HG], [0, D]], channel_multiplier=1))
            step(nc.gpsimd.affine_select(out=b4, in_=b4, compare_op=ALU.is_ge, fill=0.0,
                                         base=D - 1, pattern=[[D, HG], [0, D]], channel_multiplier=-1))
            nc.gpsimd.memset(z[:, :, C:C + 1], 1.0).then_inc(pool_const, 1)
            pool.wait_ge(in_x, 16)
            pool.wait_ge(in_bias, 48)
            step(nc.gpsimd.tensor_tensor(br_sb[:, :], br_sb[:, :], bproj_sb[:, :], ALU.add))
            for t in range(T):
                ins = nc.gpsimd.tensor_tensor(xb[:, t, :], x_sb[:, t, :], br_sb[:, :], ALU.add)
            ins.then_inc(xb_ready, 1)

        @block.scalar
        def _(act):
            act.dma_start(x_sb[:, :, :], x.rearrange("(t p) c -> p t c", p=TP)).then_inc(in_x, 16)
            act.wait_ge(var_ready, 1)
            nc.scalar.activation(rstd[:, :], rstd[:, :], ACT.Sqrt).then_inc(std_ready, 1)
            for c in range(KC):
                act.wait_ge(xT_ps, c + 1)
                nc.scalar.copy(tiles(xnT[:, c, :]), wide(2 * c)).then_inc(xT_ready, 1)
            for t in range(T):
                act.wait_ge(qkv_ps, t + 1)
                nc.scalar.copy(qk[:, t, :], ps[0:TP, 7, :])
                nc.scalar.activation(sq[:, t, :], ps[0:TP, 7, :], ACT.Square)
                nc.scalar.copy(v[:, t, :], ps[0:TP, 4 + t % 2, 0:C])
                if t == 0:
                    act.wait_ge(pool_const, 2)
                nc.scalar.copy(z[:, t, 0:C], ps[0:TP, 4 + t % 2, C:2 * C]).then_inc(qkv_copied, 1)
            act.wait_ge(norm_sq, 1)
            nc.scalar.activation(nrm[:, 0, :, :], nrm[:, 0, :, :], ACT.Sqrt, scale=SC2)
            nc.scalar.activation(nrm[:, 1, :, :], nrm[:, 1, :, :], ACT.Sqrt).then_inc(norm_sd, 1)
            act.wait_ge(A_done, 1)
            for s in range(2):
                nc.scalar.copy(AT[:, s, 0:4 * TP], ps[0:TP, s, 0:4 * TP])
            nc.scalar.copy(AT[:, 4, 4 * TP:N], ps[0:TP, 6, 0:TP]).then_inc(A_copied, 1)
            for c in range(4):
                act.wait_ge(qkT_ps, c + 1)
                nc.scalar.copy(tiles(qkT[:, c, :]), wide(2 * c)).then_inc(qkT_copied, 1)
            for u, (hg, hf, m, pr) in enumerate(units):
                lo, hi = HALF[hf]
                w = hi - lo
                act.wait_ge(s_ps, u + 1)
                if u >= NGB:
                    act.wait_ge(g_used, (u - NGB) // 2 + 1)
                b = 2 * (u % SLOTS)
                nc.scalar.activation(g[:, u % NGB, :, 0:w], ps[0:TP, b:b + 2, 0:w], ACT.Square,
                                     bias=sc2_col[0:TP, :]).then_inc(g_ready, 1)
            act.wait_ge(var_ready, 2)
            nc.scalar.activation(rstd[:, :], rstd[:, :], ACT.Sqrt).then_inc(std_ready, 1)
            for c in range(KC):
                act.wait_ge(xT_ps, KC + c + 1)
                nc.scalar.copy(tiles(x2nT[:, c, :]), wide(2 * c)).then_inc(xT_ready, 1)
            act.wait_ge(in_gate, 48)
            for k in range(KH):
                act.wait_ge(f_ps, k + 1)
                nc.scalar.activation(hT[:, k, :], psf[:, 1024 * (k % 2):1024 * (k % 2) + N], ACT.Gelu,
                                     bias=b1_sb[:, k:k + 1]).then_inc(h_ready, 1)
            act.wait_ge(ex_in, 1)
            nc.scalar.activation(ex[:, :, :], lg[:, :, :], ACT.Exp).then_inc(ex_ready, 1)

        @block.vector
        def _(dve):
            made = [0]

            def step(ins):
                made[0] += 1
                ins.then_inc(dve_chain, 1)
                dve.wait_ge(dve_chain, made[0])

            step(nc.vector.memset(sc2_col[:, :], SC2))
            dve.wait_ge(in_e, 32)
            nc.vector.tensor_copy(src_f[:, :], src_i[:, :])
            step(nc.vector.tensor_copy(dst_f[:, :], dst_i[:, :]))
            dve.wait_ge(pool_chain, 2)
            step(nc.vector.tensor_tensor(ge, dst_f[:, None, :].broadcast_to([TP, T + 1, NCH]),
                                         thr[:, :, None].broadcast_to([TP, T + 1, NCH]), ALU.is_ge))
            step(nc.vector.tensor_tensor(inr, ge[:, 0:T, :], ge[:, 1:T + 1, :], ALU.subtract))
            nc.vector.tensor_reduce(in_tile[:, :, :], inr.rearrange("p k (g j) -> p k g j", j=GC),
                                    AX.X, ALU.add).then_inc(flag_rows, 1)
            dve.wait_ge(in_x, 16)
            for t in range(T):
                step(nc.vector.bn_stats(bn[:, t, :], x_sb[:, t, :]))
                step(nc.vector.bn_aggr(mv[:, t, :], bn[:, t, :]))
            nc.vector.tensor_scalar(rstd[:, :], mv[:, :, 1], LN_EPS, None, ALU.add).then_inc(var_ready, 1)
            dve.wait_ge(flag_sum, 1)
            dve.wait_ge(pool_chain, 2 + T)
            step(nc.vector.tensor_scalar(flag_f[:, :, :], ps[0:1, 6, 0:T * NG].rearrange(
                "p (k g) -> p k g", k=T), 0.0, None, ALU.is_gt))
            step(nc.vector.tensor_tensor(flag_f[:, :, :], flag_f[:, :, :],
                                         bits[:, :, None].broadcast_to([1, T, NG]), ALU.mult))
            step(nc.vector.tensor_reduce(flag_g[:, :], flag_f[:, :, :].rearrange("p k g -> p g k"),
                                         AX.X, ALU.add))
            nc.vector.tensor_copy(flags[:, :], flag_g[:, :]).then_inc(flags_ready, 1)
            dve.wait_ge(std_ready, 1)
            step(nc.vector.reciprocal(rstd[:, :], rstd[:, :]))
            for t in range(T):
                ins = nc.vector.tensor_scalar(xn[:, t, :], x_sb[:, t, :], mv[:, t, 0:1], rstd[:, t:t + 1],
                                              ALU.subtract, ALU.mult)
            ins.then_inc(xn_ready, 1)
            with dve.Fori(0, NG // 2) as i:
                for b in range(2):
                    dve.wait_ge(oh_free, 2 * i + b + 1)
                    for j in range(GC):
                        col = i * (2 * GC) + (b * GC + j)
                        nc.vector.tensor_scalar(oh[:, b, 0, j, :], node_ids[:, :], src_f[:, bass.ds(col, 1)], None,
                                                ALU.is_equal)
                        ins = nc.vector.tensor_scalar(oh[:, b, 1, j, :], node_ids[:, :], dst_f[:, bass.ds(col, 1)],
                                                      None, ALU.is_equal)
                    ins.then_inc(oh_ready, 1)
            dve.wait_ge(qkv_copied, T)
            for w in range(2):
                ins = nc.vector.tensor_reduce(
                    nrm[:, w, :, :], sq[:, :, w * C:(w + 1) * C].rearrange("p t (h d) -> p t h d", d=D),
                    AX.X, ALU.add)
            ins.then_inc(norm_sq, 1)
            dve.wait_ge(norm_sd, 1)
            step(nc.vector.tensor_scalar(nrm[:, :, :, :], nrm[:, :, :, :], NORM_EPS, None, ALU.max))
            step(nc.vector.reciprocal(nrm[:, :, :, :], nrm[:, :, :, :]))
            dve.wait_ge(in_bias, 48)
            step(nc.vector.scalar_tensor_tensor(nrm[:, 0, :, :], nrm[:, 0, :, :], SC2,
                                                temp_sb[:, None, :].broadcast_to([TP, T, H]), ALU.mult, ALU.mult))
            step(nc.vector.tensor_scalar(nrm[:, 1, :, :], nrm[:, 1, :, :], SC, None, ALU.mult))
            for t in range(T):
                for w in range(2):
                    q3 = qk[:, t, w * C:(w + 1) * C].rearrange("p (h d) -> p h d", d=D)
                    ins = nc.vector.tensor_tensor(q3, q3, nrm[:, w, t, :, None].broadcast_to([TP, H, D]), ALU.mult)
            ins.then_inc(qk_scaled, 1)
            dve.wait_ge(A_done, 1)
            for s in range(2, T):
                nc.vector.tensor_copy(AT[:, s, 0:4 * TP], ps[0:TP, s, 0:4 * TP])
            for s in range(4):
                ins = nc.vector.tensor_copy(AT[:, s, 4 * TP:N], ps[0:TP, 5, TP * s:TP * (s + 1)])
            ins.then_inc(A_copied, 1)
            dve.wait_ge(m_ps, 1)
            for hg in range(2):
                nc.vector.tensor_tensor(MA[:, hg, :], ps[:, hg, 0:P], blk[:, :], ALU.mult)
                nc.vector.tensor_scalar(ks[:, hg:hg + 1], ps[:, hg, P:P + 1], 2 * SC2, None, ALU.mult)
                ins = nc.vector.tensor_scalar(vs[:, hg:hg + 1], ps[:, 2 + hg, 0:1], SC2 * SC2, None, ALU.mult)
            ins.then_inc(m_ready, 1)
            dve.wait_ge(dve_chain, made[0])
            dve.wait_ge(m_ready, 1)
            for hg in range(2):
                dve.wait_ge(u_ps, hg + 1)
                nc.vector.scalar_tensor_tensor(uq[:, hg, :], psf[:, 1024 * (2 + hg):1024 * (2 + hg) + N],
                                               ks[:, hg:hg + 1], qkT[:, hg, :], ALU.add, ALU.mult
                                               ).then_inc(u_ready, 1)
            for hg in range(2):
                dve.wait_ge(n_ps, hg + 1)
                step(nc.vector.tensor_scalar(rn[:, hg, :], psf[:, 1024 * hg:1024 * hg + N],
                                             2.0 * N * SC2 * SC2, None, ALU.add))
                nc.vector.reciprocal(rn[:, hg, :], rn[:, hg, :]).then_inc(n_ready, 1)
            dve.wait_ge(n_ready, 2)
            for k in range(4):
                hg, (lo, hi) = k // 2, HALF[k % 2]
                dve.wait_ge(g_used, T * (k + 1))
                nc.vector.scalar_tensor_tensor(yT[:, hg, lo:hi], ps[:, 6 + k % 2, 0:hi - lo], vs[:, hg:hg + 1],
                                               rn[:, hg, lo:hi], ALU.add, ALU.mult).then_inc(y_ready, 1)
            dve.wait_ge(xb_ready, 1)
            for t in range(T):
                dve.wait_ge(rp_ps, t + 1)
                a = ps[0:TP, 2 * (t % 2), :]
                r = ps[0:TP, 2 * (t % 2) + 1, :]
                step(nc.vector.tensor_scalar(cnt[:, t:t + 1], a[:, C:C + 1], 1.0, None, ALU.max))
                step(nc.vector.reciprocal(cnt[:, t:t + 1], cnt[:, t:t + 1]))
                step(nc.vector.scalar_tensor_tensor(x2[:, t, :], a[:, 0:C], cnt[:, t:t + 1], xb[:, t, :],
                                                    ALU.mult, ALU.add))
                nc.vector.tensor_tensor(x2[:, t, :], x2[:, t, :], r[:, 0:C], ALU.add).then_inc(x2_ready, 1)
                dve.wait_ge(x2_ready, t + 1)
                step(nc.vector.bn_stats(bn[:, t, :], x2[:, t, :]))
                step(nc.vector.bn_aggr(mv[:, t, :], bn[:, t, :]))
            nc.vector.tensor_scalar(rstd[:, :], mv[:, :, 1], LN_EPS, None, ALU.add).then_inc(var_ready, 1)
            dve.wait_ge(std_ready, 2)
            step(nc.vector.reciprocal(rstd[:, :], rstd[:, :]))
            for t in range(T):
                ins = nc.vector.tensor_scalar(x2n[:, t, :], x2[:, t, :], mv[:, t, 0:1], rstd[:, t:t + 1],
                                              ALU.subtract, ALU.mult)
            ins.then_inc(xn_ready, 1)
            dve.wait_ge(lg_ps, 1)
            dve.wait_ge(in_gate, 48)
            step(nc.vector.tensor_tensor(lg[:, :, :], ps[0:TP, 4, 0:T * E].rearrange("p (t e) -> p t e", e=E),
                                         bg_sb[:, None, :].broadcast_to([TP, T, E]), ALU.add))
            step(nc.vector.tensor_reduce(mx[:, :], lg[:, :, :], AX.X, ALU.max))
            mxb = mx[:, :, None].broadcast_to([TP, T, E])
            nc.vector.tensor_tensor(lg[:, :, :], lg[:, :, :], mxb, ALU.subtract).then_inc(ex_in, 1)
            dve.wait_ge(ex_in, 1)
            step(nc.vector.scalar_tensor_tensor(eq[:, :, :], lg[:, :, :], 0.0,
                                                erank[:, None, :].broadcast_to([TP, T, E]),
                                                ALU.is_equal, ALU.mult))
            step(nc.vector.tensor_reduce(rk[:, :], eq[:, :, :], AX.X, ALU.max))
            step(nc.vector.tensor_tensor(eq[:, :, :], eq[:, :, :], rk[:, :, None].broadcast_to([TP, T, E]),
                                         ALU.is_equal))
            dve.wait_ge(ex_ready, 1)
            step(nc.vector.tensor_reduce(se[:, :], ex[:, :, :], AX.X, ALU.add))
            step(nc.vector.reciprocal(se[:, :], se[:, :]))
            nc.vector.tensor_tensor(selp[:, :, :], eq[:, :, :], se[:, :, None].broadcast_to([TP, T, E]),
                                    ALU.mult).then_inc(sel_ready, 1)
            dve.wait_ge(sel_ready, 1)
            dve.wait_ge(selT_ps, 1)
            nc.vector.tensor_copy(tiles(selT[:, :]), wide(5)[0:E]).then_inc(selT_ready, 1)
            for t in range(T):
                dve.wait_ge(bd_ps, t + 1)
                nc.vector.tensor_tensor(x2[:, t, :], x2[:, t, :], ps[0:TP, t, 0:C], ALU.add
                                        ).then_inc(acc_ready, 1)
            with dve.Fori(0, E) as e:
                for t in range(T):
                    dve.wait_ge(e_ps, e * T + (t + 1))
                    dve.wait_ge(acc_ready, e * T + (t + 1))
                    nc.vector.scalar_tensor_tensor(x2[:, t, :], ps[0:TP, t, 0:C],
                                                   selp[:, t, bass.ds(e, 1)], x2[:, t, :],
                                                   ALU.mult, ALU.add).then_inc(acc_ready, 1)
        @block.tensor
        def _(pe):
            mm = nc.tensor.matmul
            pe.wait_ge(pool_const, 1)
            pe.wait_ge(flag_rows, 1)
            mm(ps[0:1, 6, 0:T * NG], ones_c[0:TP, 0:1], in_tile[:, :, :].rearrange("p k g -> p (k g)"),
               start=True, stop=True).then_inc(flag_sum, 1)

            pe.wait_ge(xn_ready, 1)
            for c in range(KC):
                for t in range(T):
                    ins = nc.tensor.transpose(wide(2 * c)[:, t, :], xn[:, t, P * c:P * (c + 1)], ident[0:TP, 0:TP])
                ins.then_inc(xT_ps, 1)
            pe.wait_ge(in_wqkv, 16)
            pe.wait_ge(in_bqkv, 16)
            pe.wait_ge(in_wlr, 16)
            pe.wait_ge(xT_ready, KC)
            for t in range(T):
                if t >= 1:
                    pe.wait_ge(qkv_copied, t)
                own = slice(TP * t, TP * (t + 1))
                for c in range(KC):
                    mm(ps[0:TP, 7, :], xnT[:, c, own], wqkv_sb[:, c, 0:2 * C], start=(c == 0), stop=False)
                mm(ps[0:TP, 7, :], ones_c[0:1, 0:TP], bqkv_sb[:, 0:2 * C], start=False, stop=True)
                b = 4 + t % 2
                for c in range(KC):
                    mm(ps[0:TP, b, 0:C], xnT[:, c, own], wqkv_sb[:, c, 2 * C:3 * C], start=(c == 0), stop=False)
                mm(ps[0:TP, b, 0:C], ones_c[0:1, 0:TP], bqkv_sb[:, 2 * C:3 * C], start=False, stop=True)
                for c in range(KC):
                    ins = mm(ps[0:TP, b, C:2 * C], xnT[:, c, own], wlr_sb[:, c, 0:C], start=(c == 0),
                             stop=(c == KC - 1))
                ins.then_inc(qkv_ps, 1)
            pe.wait_ge(qkv_copied, T)
            pe.wait_ge(flags_ready, 1)
            for b in range(7):
                mm(ps[:, b, :], zeros[:, 0:P], zeros[:, :], start=True, stop=False, skip_group_check=True)
            pe.sem_inc(oh_free, 2)
            with pe.Fori(0, NG // 2) as i:
                for b in range(2):
                    has = pe.value_load(flags[0:1, bass.ds(i * 2 + b, 1)], min_val=0, max_val=2 ** T - 1)
                    pe.wait_ge(oh_ready, 2 * i + b + 1)
                    for t in range(T):
                        with pe.If((has >> t) & 1):
                            for j in range(GC):
                                for s in range(T):
                                    mm(a_block(s, t), oh[:, b, 0, j, TP * s:TP * s + P],
                                       oh[:, b, 1, j, TP * t:TP * (t + 1)], start=False, stop=False,
                                       skip_group_check=True)
                    mm(ps[:, 6, 256:384], zeros[:, 0:P], zeros[:, 0:P], start=False, stop=False,
                       skip_group_check=True).then_inc(oh_free, 1)
            for b in range(7):
                ins = mm(ps[:, b, 0:2], zeros[:, 0:P], zeros[:, 0:2], start=False, stop=True, skip_group_check=True)
            ins.then_inc(A_done, 1)
            pe.wait_ge(qk_scaled, 1)
            pe.wait_ge(A_copied, 2)
            for c in range(4):
                for t in range(T):
                    ins = nc.tensor.transpose(wide(2 * c)[:, t, :], qk[:, t, P * c:P * (c + 1)], ident[0:TP, 0:TP])
                ins.then_inc(qkT_ps, 1)
            pe.wait_ge(qkT_copied, 4)
            pe.wait_ge(pool_const, 2)
            for hg in range(2):
                k_h = slice(C + P * hg, C + P * (hg + 1))
                for t in range(T):
                    mm(ps[:, hg, 0:P], qk[:, t, k_h], qk[:, t, k_h], start=(t == 0), stop=(t == T - 1))
                for t in range(T):
                    mm(ps[:, hg, P:P + 1], qk[:, t, k_h], ones_c[0:TP, 0:1], start=(t == 0), stop=(t == T - 1))
                for t in range(T):
                    ins = mm(ps[:, 2 + hg, 0:1], v[:, t, P * hg:P * (hg + 1)], ones_c[0:TP, 0:1],
                             start=(t == 0), stop=(t == T - 1))
            ins.then_inc(m_ps, 1)
            pe.wait_ge(m_ready, 1)
            for hg in range(2):
                for lo, hi in SPLIT:
                    ins = mm(psf[:, 1024 * (2 + hg) + lo:1024 * (2 + hg) + hi], MA[:, hg, :], qkT[:, hg, lo:hi],
                             start=True, stop=True)
                ins.then_inc(u_ps, 1)
            for hg in range(2):
                pe.wait_ge(u_ready, hg + 1)
                for lo, hi in SPLIT:
                    ins = mm(psf[:, 1024 * hg + lo:1024 * hg + hi], blk[:, :], uq[:, hg, lo:hi],
                             start=True, stop=True)
                ins.then_inc(n_ps, 1)
            pe.wait_ge(n_ready, 2)

            def scores(u):
                hg, hf, m, pr = units[u]
                lo, hi = HALF[hf]
                if u >= SLOTS:
                    pe.wait_ge(g_ready, u - SLOTS + 1)
                for i in range(2):
                    r = D * (2 * pr + i)
                    ins = mm(ps[0:TP, 2 * (u % SLOTS) + i, 0:hi - lo], qkT[r:r + D, 2 + hg, TP * m:TP * (m + 1)],
                             qkT[r:r + D, hg, lo:hi], start=True, stop=True)
                ins.then_inc(s_ps, 1)

            def values(u2):
                hg, hf, m, _ = units[2 * u2]
                lo, hi = HALF[hf]
                k = 2 * hg + hf
                pe.wait_ge(g_ready, 2 * u2 + 2)
                if m == 0 and k >= 2:
                    pe.wait_ge(y_ready, k - 1)
                for pr in range(2):
                    for i in range(2):
                        h = 2 * pr + i
                        ins = mm(ps[D * h:D * (h + 1), 6 + k % 2, 0:hi - lo],
                                 v[:, m, P * hg + D * h:P * hg + D * (h + 1)],
                                 g[:, (2 * u2 + pr) % NGB, i, 0:hi - lo], start=(m == 0), stop=(m == T - 1),
                                 tile_position=(0, D * h), skip_group_check=True)
                ins.then_inc(g_used, 1)

            U2 = len(units) // 2
            scores(0)
            scores(1)
            for u2 in range(U2):
                if u2 + 1 < U2:
                    scores(2 * u2 + 2)
                    scores(2 * u2 + 3)
                values(u2)
            pe.wait_ge(g_ready, len(units))
            pe.wait_ge(y_ready, 4)
            pe.wait_ge(in_wproj, 16)
            for t in range(T):
                if t >= 2:
                    pe.wait_ge(x2_ready, t - 1)
                own = slice(TP * t, TP * (t + 1))
                b = 2 * (t % 2)
                for s in range(T):
                    mm(ps[0:TP, b, 0:C + 1], AT[:, s, own], z[:, s, :], start=(s == 0), stop=(s == T - 1))
                for c in range(KC):
                    mm(ps[0:TP, b + 1, 0:C], xnT[:, c, own], wlr_sb[:, c, C:2 * C], start=(c == 0), stop=False)
                for c in range(KC):
                    ins = mm(ps[0:TP, b + 1, 0:C], yT[:, c, own], wproj_sb[:, c, :], start=False,
                             stop=(c == KC - 1))
                ins.then_inc(rp_ps, 1)
            pe.wait_ge(xn_ready, 2)
            for c in range(KC):
                for t in range(T):
                    ins = nc.tensor.transpose(wide(2 * c)[:, t, :], x2n[:, t, P * c:P * (c + 1)], ident[0:TP, 0:TP])
                ins.then_inc(xT_ps, 1)
            pe.wait_ge(in_w1, 16)
            pe.wait_ge(xT_ready, 2 * KC)
            for k in range(KH):
                if k >= 2:
                    pe.wait_ge(h_ready, k - 1)
                for lo, hi in SPLIT:
                    for c in range(KC):
                        ins = mm(psf[:, 1024 * (k % 2) + lo:1024 * (k % 2) + hi], w1_sb[:, c, P * k:P * (k + 1)],
                                 x2nT[:, c, lo:hi], start=(c == 0), stop=(c == KC - 1))
                ins.then_inc(f_ps, 1)
            pe.wait_ge(in_gate, 48)
            pe.wait_ge(h_ready, KH)
            for t in range(T):
                for k in range(KH):
                    ins = mm(ps[0:TP, 4, E * t:E * (t + 1)], hT[:, k, TP * t:TP * (t + 1)], wg_sb[:, k, :],
                             start=(k == 0), stop=(k == KH - 1))
            ins.then_inc(lg_ps, 1)
            pe.wait_ge(sel_ready, 1)
            for t in range(T):
                ins = nc.tensor.transpose(wide(5)[0:E, t, :], selp[:, t, :], ident[0:TP, 0:TP])
            ins.then_inc(selT_ps, 1)
            pe.wait_ge(selT_ready, 1)
            pe.wait_ge(in_bd, 16)
            for t in range(T):
                mm(ps[0:TP, t, 0:C], selT[:, TP * t:TP * (t + 1)], bd_sb[:, :],
                   start=True, stop=True).then_inc(bd_ps, 1)
            pe.wait_ge(in_wd, 16 * E)
            with pe.Fori(0, E) as e:
                for t in range(T):
                    pe.wait_ge(acc_ready, e * T + (t + 1))
                    for k in range(KH):
                        ins = mm(ps[0:TP, t, 0:C], hT[:, k, TP * t:TP * (t + 1)], wd_sb[:, bass.ds(e, 1), k, :],
                                 start=(k == 0), stop=(k == KH - 1))
                    ins.then_inc(e_ps, 1)


_OUT = (625, 256)


def kernel(**inputs):
    import numpy as np
    import concourse.bacc as bacc
    from concourse.bass_utils import run_bass_kernel_spmd

    a = {k: np.asarray(v) for k, v in inputs.items()}

    def rows(w, k):
        return np.ascontiguousarray(w.reshape(k, 128, -1).transpose(1, 0, 2))

    tp = 125
    arrays = {
        "x": np.ascontiguousarray(a["x"]),
        "src": np.ascontiguousarray(a["src"].reshape(-1, tp).T),
        "dst": np.ascontiguousarray(a["dst"].reshape(-1, tp).T),
        "w_qkv": rows(a["L0_mix_Wqkv"].T, 2),
        "b_qkv": a["L0_mix_bqkv"].reshape(1, -1),
        "w_lr": rows(np.concatenate([a["L0_gnn_W_l"].T, a["L0_gnn_W_r"].T], axis=1), 2),
        "b_r": a["L0_gnn_b_r"].reshape(1, -1),
        "w_proj": rows(a["L0_mix_Wproj"].T, 2),
        "b_proj": a["L0_mix_bproj"].reshape(1, -1),
        "temp": a["L0_mix_temperature"].reshape(1, -1),
        "w1": rows(a["L0_ffn_W1"], 2),
        "b1": np.ascontiguousarray(a["L0_ffn_b1"].reshape(8, 128).T),
        "wg": rows(a["L0_ffn_Wg"], 8),
        "bg": a["L0_ffn_bg"].reshape(1, -1),
        "wd": np.ascontiguousarray(a["L0_ffn_Wd"].reshape(8, 8, 128, 256).transpose(2, 0, 1, 3)),
        "bd": np.ascontiguousarray(a["L0_ffn_bd"]),
    }
    nc = bacc.Bacc("TRN2", target_bir_lowering=False, num_devices=1)
    args = [nc.dram_tensor(f"in_{n}", v.shape, mybir.dt.from_np(v.dtype), kind="ExternalInput").ap()
            for n, v in arrays.items()]
    out = nc.dram_tensor("out_0", _OUT, F32, kind="ExternalOutput").ap()
    gps_layer(nc, *args, out)
    r = run_bass_kernel_spmd(nc, [{f"in_{n}": v for n, v in arrays.items()}], core_ids=[0])
    return r.results[0]["out_0"]
```

```python
from contextlib import ExitStack

import concourse.bass as bass
from concourse import mybir

F32 = mybir.dt.float32
F16 = mybir.dt.float16
BF16 = mybir.dt.bfloat16
I32 = mybir.dt.int32
U32 = mybir.dt.uint32
ALU = mybir.AluOpType
ACT = mybir.ActivationFunctionType
AX = mybir.AxisListType

P = 128
LN_EPS = 1e-5
NORM_EPS = 1e-12


def gps_layer(nc, x, src, dst, w_qkv, b_qkv, w_lr, b_r, w_proj, b_proj, temp,
              w1, b1, wg, bg, wd, bd, rows_sorted, out):
    N, C = x.shape
    TP = 125
    T = N // TP
    KC = C // P
    NCH = src.shape[1]
    GC = 10
    NG = NCH // GC
    OHW = TP * (T - 1) + P
    H = temp.shape[1]
    D = C // H
    HG = P // D
    SC2 = float(D) ** 0.5
    SC = SC2 ** 0.5
    HID = w1.shape[2]
    KH = HID // P
    E = bg.shape[1]
    HALF = [(0, (N + 1) // 2), ((N + 1) // 2, N)]
    HW = HALF[0][1]
    BANK = 512
    SPLIT = [(0, BANK), (BANK, N)]
    assert N == T * TP and NG * GC == NCH and NG % 2 == 0 and H == 2 * HG

    with ExitStack() as ctx:
        def sb(name, shape, dt=F32):
            return ctx.enter_context(nc.sbuf_tensor(name, shape, dt))

        def sem(name):
            return ctx.enter_context(nc.semaphore(name))

        ps = ctx.enter_context(nc.psum_tensor("ps", [P, 8, BANK], F32))
        psf = ps[:, :, :].rearrange("p b n -> p (b n)")

        x_sb = sb("x_sb", [TP, T, C])
        src_i = sb("src_i", [TP, NCH], I32)
        dst_i = sb("dst_i", [TP, NCH], I32)
        wqkv_sb = sb("wqkv_sb", [P, KC, 3 * C])
        bqkv_sb = sb("bqkv_sb", [TP, 3 * C])
        wlr_sb = sb("wlr_sb", [P, KC, 2 * C])
        wproj_sb = sb("wproj_sb", [P, KC, C])
        br_sb = sb("br_sb", [TP, C])
        bproj_sb = sb("bproj_sb", [TP, C])
        temp_sb = sb("temp_sb", [TP, H])
        w1_sb = sb("w1_sb", [P, KC, HID])
        b1_sb = sb("b1_sb", [P, KH])
        wg_sb = sb("wg_sb", [P, KH, E])
        bg_sb = sb("bg_sb", [TP, E])
        WD = E * KH * C
        OH = 2 * 2 * GC * OHW // 2
        BIG = 2 * KH * N
        LATE = -(-(OH - BIG) // (KH * C))
        mem = sb("mem", [P, WD + BIG])
        wd_sb = mem[:, 0:WD].rearrange("p (e k c) -> p e k c", e=E, k=KH)
        big = mem[:, WD:WD + BIG]
        bd_sb = sb("bd_sb", [E, C])
        ident = sb("ident", [P, P])
        blk = sb("blk", [P, P])
        identh = sb("identh", [P, P], F16)
        node_ids = sb("node_ids", [TP, OHW], F16)
        ids_m1 = sb("ids_m1", [TP, OHW], F16)
        ones_c = sb("ones_c", [P, P])
        sc2_col = sb("sc2_col", [P, 1])
        zeros = sb("zeros", [TP, BANK], BF16)
        thr = sb("thr", [TP, T + 1])
        bits = sb("bits", [1, T])
        erank = sb("erank", [TP, E])
        src_f = sb("src_f", [TP, NCH])
        dst_f = sb("dst_f", [TP, NCH])
        half_dst = sb("half_dst", [TP, NCH])
        in_tile = sb("in_tile", [TP, T, NG])
        flag_f = sb("flag_f", [1, T, NG])
        flag_g = sb("flag_g", [1, NG])
        flags = sb("flags", [1, NG], I32)
        at_sb = sb("at_sb", [P, T * N])
        qk_sb = sb("qk_sb", [P, 2560])
        oh = mem[0:TP, WD + BIG - OH:WD + BIG].bitcast(BF16).rearrange("p (b w j n) -> p b w j n", b=2, w=2, j=GC)
        ge = big[0:TP, 0:(T + 1) * NCH].rearrange("p (k n) -> p k n", k=T + 1)
        inr = big[0:TP, (T + 1) * NCH:(2 * T + 1) * NCH].rearrange("p (k n) -> p k n", k=T)
        hT = big[:, 0:KH * N].rearrange("p (k n) -> p k n", k=KH)
        st = big[:, 0:H * N].bitcast(F16).rearrange("p (w h n) -> p w h n", w=2, h=H)
        qT = big[:, H * N:(H + 2) * N].rearrange("p (k n) -> p k n", k=2)
        rn = big[:, (H + 2) * N:(H + 4) * N].rearrange("p (k n) -> p k n", k=2)
        RW = rows_sorted.shape[1]
        row = sb("row", [TP, T, RW])
        x2 = row[:, :, 0:C]
        x2n = row[:, :, C:2 * C]
        selp = row[:, :, 2 * C:2 * C + E]
        node = row[:, :, 2 * C + E]
        bn = sb("bn", [TP, T, 6])
        mv = sb("mv", [TP, T, 2])
        rstd = sb("rstd", [TP, T])
        xn = x2n
        xnT = sb("xnT", [P, KC, N])
        xb = sb("xb", [TP, T, C])
        qk = qk_sb[0:TP, :].rearrange("p (t c) -> p t c", t=T)
        sq = at_sb[0:TP, 0:T * 2 * C].rearrange("p (t c) -> p t c", t=T)
        hl = row[:, :, 0:2 * C].bitcast(F16).rearrange("p t (w h i d) -> p t w h i d", w=2, h=H, i=2)
        v = sb("v", [TP, T, C])
        z = sb("z", [TP, T, C + 1])
        nrm = sb("nrm", [TP, 2, T, H])
        MA = sb("MA", [P, 2, P])
        ks = sb("ks", [P, 2])
        vs = sb("vs", [P, 2])
        NGB = 4
        g = qk_sb[0:TP, 0:NGB * 2 * HW].rearrange("p (b i n) -> p b i n", b=NGB, i=2)
        yT = sb("yT", [P, 2, N])
        uq = yT
        PW = N + N % 2
        perm = at_sb[0:TP, 0:T * PW // 2].bitcast(BF16).rearrange("p (t n) -> p t n", t=T)
        xs = qk_sb[0:TP, 0:3 * T * C // 2].bitcast(BF16).rearrange("p (i t c) -> p i t c", i=3, t=T)
        AT = at_sb[0:TP, :].rearrange("p (s n) -> p s n", s=T)
        cnt = sb("cnt", [TP, T])
        x2nT = xnT
        lg = sb("lg", [TP, T, E])
        mx = sb("mx", [TP, T])
        ex = sb("ex", [TP, T, E])
        se = sb("se", [TP, T])
        eq = sb("eq", [TP, T, E])
        rk = sb("rk", [TP, T])
        tri = sb("tri", [TP, TP])
        tot = sb("tot", [TP, E, T])
        inc = sb("inc", [TP, E, T])
        at_e = sb("at_e", [TP, E, T])
        pos_f = sb("pos_f", [TP, T])
        pos = sb("pos", [TP, T], U32)
        node_u = sb("node_u", [TP, T], U32)
        eflag_f = sb("eflag_f", [1, T, E])
        eflag_g = sb("eflag_g", [1, E])
        eflags = sb("eflags", [1, E], I32)
        selT = sb("selT", [E, N])

        in_e = sem("in_e")
        in_x = sem("in_x")
        in_wqkv = sem("in_wqkv")
        in_bqkv = sem("in_bqkv")
        in_wlr = sem("in_wlr")
        in_bias = sem("in_bias")
        in_wproj = sem("in_wproj")
        in_w1 = sem("in_w1")
        in_gate = sem("in_gate")
        in_wd = sem("in_wd")
        in_bd = sem("in_bd")
        pool_const = sem("pool_const")
        pool_chain = sem("pool_chain")
        dve_chain = sem("dve_chain")
        flag_rows = sem("flag_rows")
        flag_sum = sem("flag_sum")
        flags_ready = sem("flags_ready")
        oh_ready = sem("oh_ready")
        steps_ready = sem("steps_ready")
        half_ready = sem("half_ready")
        st_ps = sem("st_ps")
        z_copied = sem("z_copied")
        sq_ready = sem("sq_ready")
        var2_ready = sem("var2_ready")
        std2_ready = sem("std2_ready")
        xn2_ready = sem("xn2_ready")
        x2T_ps = sem("x2T_ps")
        x2T_ready = sem("x2T_ready")
        xs_ready = sem("xs_ready")
        perm_ready = sem("perm_ready")
        A_left = sem("A_left")
        st_copied_a = sem("st_copied_a")
        st_copied_v = sem("st_copied_v")
        hl_ready = sem("hl_ready")
        oh_free = sem("oh_free")
        var_ready = sem("var_ready")
        std_ready = sem("std_ready")
        xn_ready = sem("xn_ready")
        xT_ps = sem("xT_ps")
        xT_ready = sem("xT_ready")
        qkv_ps = sem("qkv_ps")
        qkv_copied = sem("qkv_copied")
        norm_sq = sem("norm_sq")
        norm_sd = sem("norm_sd")
        scales_ready = sem("scales_ready")
        qkT_ps = sem("qkT_ps")
        qkT_copied = sem("qkT_copied")
        A_done = sem("A_done")
        A_copied = sem("A_copied")
        xb_ready = sem("xb_ready")
        m_ps = sem("m_ps")
        m_ready = sem("m_ready")
        u_ps = sem("u_ps")
        u_ready = sem("u_ready")
        n_ps = sem("n_ps")
        n_ready = sem("n_ready")
        s_ps = sem("s_ps")
        g_ready = sem("g_ready")
        g_used = sem("g_used")
        y_ready = sem("y_ready")
        rp_ps = sem("rp_ps")
        x2_ready = sem("x2_ready")
        f_ps = sem("f_ps")
        h_ready = sem("h_ready")
        lg_ps = sem("lg_ps")
        ex_in = sem("ex_in")
        ex_ready = sem("ex_ready")
        rank_in = sem("rank_in")
        rank_ps = sem("rank_ps")
        pos_ready = sem("pos_ready")
        rows_sent = sem("rows_sent")
        rows_back = sem("rows_back")
        esum_ps = sem("esum_ps")
        eflags_ready = sem("eflags_ready")
        selT_ps = sem("selT_ps")
        selT_ready = sem("selT_ready")
        bd_ps = sem("bd_ps")
        acc_ready = sem("acc_ready")
        e_ps = sem("e_ps")
        out_sent = sem("out_sent")

        AW = TP + 1
        def a_block(s, t):
            return ps[:, s, AW * t:AW * (t + 1)] if t < 4 else ps[:, 5 + s // 4, AW * (s % 4):AW * (s % 4 + 1)]

        def count_parts():
            for s in range(T):
                yield tiles(AT[:, s, 0:4 * TP]), ps[0:TP, s, 0:4 * AW].rearrange("p (t n) -> p t n", n=AW)
            yield AT[:, 0:4, 4 * TP:N], ps[0:TP, 5, 0:4 * AW].rearrange("p (t n) -> p t n", n=AW)
            yield AT[:, 4, 4 * TP:N], ps[0:TP, 6, 0:AW]

        ACT_STEPS = (5, 6)

        def wide(b):
            return psf[:, BANK * b:BANK * b + T * P].rearrange("p (t n) -> p t n", n=P)[:, :, 0:TP]

        def wide_h(b):
            return ps[:, b, :].bitcast(F16)[:, 0:T * P].rearrange("p (t n) -> p t n", n=P)[:, :, 0:TP]

        def x2T_bank(t):
            return ps[:, 4 + t % 4, 0:KC * TP].rearrange("p (c n) -> p c n", c=KC)

        ST_BANKS = (6, 7, 4, 5)

        def tiles(row):
            return row.rearrange("p (t n) -> p t n", n=TP)

        units = [(hg, hf, m, pr) for hg in range(2) for hf in range(2) for m in range(T) for pr in range(2)]
        SLOTS = 3

        block = ctx.enter_context(nc.Block())

        @block.sync
        def _(sp):
            sp.dma_start(src_i[:, :], src).then_inc(in_e, 16)
            sp.dma_start(dst_i[:, :], dst).then_inc(in_e, 16)
            sp.dma_start(wqkv_sb[:, :, :], w_qkv).then_inc(in_wqkv, 16)
            sp.dma_start(bqkv_sb[:, :], b_qkv.partition_broadcast(TP)).then_inc(in_bqkv, 16)
            sp.dma_start(wlr_sb[:, :, :], w_lr).then_inc(in_wlr, 16)
            sp.dma_start(br_sb[:, :], b_r.partition_broadcast(TP)).then_inc(in_bias, 16)
            sp.dma_start(bproj_sb[:, :], b_proj.partition_broadcast(TP)).then_inc(in_bias, 16)
            sp.dma_start(temp_sb[:, :], temp.partition_broadcast(TP)).then_inc(in_bias, 16)
            sp.dma_start(wproj_sb[:, :, :], w_proj).then_inc(in_wproj, 16)
            sp.dma_start(w1_sb[:, :, :], w1).then_inc(in_w1, 16)
            sp.dma_start(b1_sb[:, :], b1).then_inc(in_gate, 16)
            sp.dma_start(wg_sb[:, :, :], wg).then_inc(in_gate, 16)
            sp.dma_start(bg_sb[:, :], bg.partition_broadcast(TP)).then_inc(in_gate, 16)
            sp.dma_start(bd_sb[:, :], bd).then_inc(in_bd, 16)
            for e in range(E):
                if e == E - LATE:
                    sp.wait_ge(A_done, 1)
                sp.dma_start(wd_sb[:, e, :, :], wd[:, e, :, :]).then_inc(in_wd, 16)
            sp.wait_ge(rows_sent, 16 * T)
            sp.dma_start(row[:, :, :], rows_sorted.rearrange("(t p) c -> p t c", p=TP)).then_inc(rows_back, 16)

        @block.gpsimd
        def _(pool):
            made = [0]

            def step(ins):
                made[0] += 1
                ins.then_inc(pool_chain, 1)
                pool.wait_ge(pool_chain, made[0])

            step(nc.gpsimd.iota(node_ids[:, :], pattern=[[1, OHW]], base=0, channel_multiplier=0,
                                allow_small_or_imprecise_dtypes=True))
            step(nc.gpsimd.iota(ids_m1[:, :], pattern=[[1, OHW]], base=-1, channel_multiplier=0,
                                allow_small_or_imprecise_dtypes=True))
            step(nc.gpsimd.iota(thr[:, :], pattern=[[TP, T + 1]], base=0, channel_multiplier=0,
                                allow_small_or_imprecise_dtypes=True))
            for t in range(T):
                step(nc.gpsimd.memset(bits[:, t:t + 1], float(2 ** t)))
            step(nc.gpsimd.memset(ones_c[:, :], 1.0))
            step(nc.gpsimd.memset(ident[:, :], 0.0))
            step(nc.gpsimd.affine_select(out=ident[:, :], in_=ident[:, :], compare_op=ALU.not_equal, fill=1.0,
                                         base=0, pattern=[[-1, P]], channel_multiplier=1))
            step(nc.gpsimd.tensor_copy(identh[:, :], ident[:, :]))
            nc.gpsimd.memset(zeros[:, :], 0.0).then_inc(pool_const, 1)
            step(nc.gpsimd.iota(erank[:, :], pattern=[[-1, E]], base=E, channel_multiplier=0,
                                allow_small_or_imprecise_dtypes=True))
            b4 = blk[:, :].rearrange("p (j d) -> p j d", d=D)
            step(nc.gpsimd.memset(blk[:, :], 1.0))
            step(nc.gpsimd.affine_select(out=b4, in_=b4, compare_op=ALU.is_ge, fill=0.0,
                                         base=0, pattern=[[-D, HG], [0, D]], channel_multiplier=1))
            step(nc.gpsimd.affine_select(out=b4, in_=b4, compare_op=ALU.is_ge, fill=0.0,
                                         base=D - 1, pattern=[[D, HG], [0, D]], channel_multiplier=-1))
            step(nc.gpsimd.memset(tri[:, :], 1.0))
            step(nc.gpsimd.affine_select(out=tri[:, :], in_=tri[:, :], compare_op=ALU.is_gt, fill=0.0,
                                         base=0, pattern=[[1, TP]], channel_multiplier=-1))
            nc.gpsimd.memset(z[:, :, C:C + 1], 1.0).then_inc(pool_const, 1)
            pool.wait_ge(in_x, 16)
            pool.wait_ge(in_bias, 48)
            step(nc.gpsimd.tensor_tensor(br_sb[:, :], br_sb[:, :], bproj_sb[:, :], ALU.add))
            for t in range(T):
                ins = nc.gpsimd.tensor_tensor(xb[:, t, :], x_sb[:, t, :], br_sb[:, :], ALU.add)
            ins.then_inc(xb_ready, 1)
            nc.gpsimd.iota(node, pattern=[[TP, T]], base=0, channel_multiplier=1,
                           allow_small_or_imprecise_dtypes=True).then_inc(pool_const, 1)
            for t in range(T):
                pool.wait_ge(scales_ready, 1)
                for w in range(2):
                    q3 = qk[:, t, w * C:(w + 1) * C].rearrange("p (h d) -> p h d", d=D)
                    ins = nc.gpsimd.tensor_tensor(q3, q3, nrm[:, w, t, :, None].broadcast_to([TP, H, D]), ALU.mult)
                step(ins)
                q4 = qk[:, t, :].rearrange("p (w h d) -> p w h d", w=2, d=D)
                for w in range(2):
                    step(nc.gpsimd.tensor_copy(hl[:, t, w, :, 0, :], q4[:, w]))
                    ins = nc.gpsimd.tensor_tensor(hl[:, t, w, :, 1, :], q4[:, w], hl[:, t, w, :, 0, :], ALU.subtract)
                ins.then_inc(hl_ready, 1)
            pool.wait_ge(pool_const, 3)
            pool.wait_ge(pos_ready, 1)
            for t in range(T):
                nc.gpsimd.indirect_dma_start(rows_sorted, bass.IndirectOffsetOnAxis(pos[:, t:t + 1], 0),
                                             row[:, t, :], None).then_inc(rows_sent, 16)
            for t in range(T):
                pool.wait_ge(acc_ready, T * E + t + 1)
                nc.gpsimd.indirect_dma_start(out, bass.IndirectOffsetOnAxis(node_u[:, t:t + 1], 0),
                                             x2[:, t, :], None).then_inc(out_sent, 16)
            pool.wait_ge(out_sent, 16 * T)

        @block.scalar
        def _(act):
            act.dma_start(x_sb[:, :, :], x.rearrange("(t p) c -> p t c", p=TP)).then_inc(in_x, 16)
            act.wait_ge(var_ready, 1)
            nc.scalar.activation(rstd[:, :], rstd[:, :], ACT.Sqrt).then_inc(std_ready, 1)
            for c in range(KC):
                act.wait_ge(xT_ps, c + 1)
                nc.scalar.copy(tiles(xnT[:, c, :]), wide(2 * c)).then_inc(xT_ready, 1)
            act.wait_ge(pool_const, 2)
            for t in range(T):
                act.wait_ge(qkv_ps, t + 1)
                nc.scalar.copy(z[:, t, 0:C], ps[0:TP, 4 + t % 2, C:2 * C]).then_inc(z_copied, 1)
                act.wait_ge(qkv_copied, t + 1)
                nc.scalar.activation(sq[:, t, :], qk[:, t, :], ACT.Square).then_inc(sq_ready, 1)
            act.wait_ge(half_ready, 1)

            def steps(first, last):
                with act.Fori(first, last) as i:
                    for b in range(2):
                        act.wait_ge(oh_free, 2 * i + b + 1)
                        for j in range(ACT_STEPS[b]):
                            col = i * (2 * GC) + (b * GC + j)
                            ins = nc.scalar.activation(oh[:, b, 1, j, :], ids_m1[:, :], ACT.Sign,
                                                       bias=half_dst[:, bass.ds(col, 1)])
                        ins.then_inc(steps_ready, 1)

            steps(0, 1)
            act.wait_ge(norm_sq, 1)
            nc.scalar.activation(nrm[:, 0, :, :], nrm[:, 0, :, :], ACT.Sqrt, scale=SC2)
            nc.scalar.activation(nrm[:, 1, :, :], nrm[:, 1, :, :], ACT.Sqrt).then_inc(norm_sd, 1)
            steps(1, NG // 2)
            act.wait_ge(A_done, 1)
            for counts, sums in count_parts():
                nc.scalar.copy(counts, sums[..., 0:TP]).then_inc(A_left, 1)
            for c in range(2):
                act.wait_ge(qkT_ps, c + 1)
                nc.scalar.copy(tiles(qT[:, c, :]), wide(2 * c)).then_inc(qkT_copied, 1)
            for n in range(0, 2 * H, 2):
                act.wait_ge(st_ps, n + 1)
                nc.scalar.copy(tiles(st[:, n % 2, n // 2, :]), wide_h(ST_BANKS[n % 4])).then_inc(st_copied_a, 1)
            for u, (hg, hf, m, pr) in enumerate(units):
                lo, hi = HALF[hf]
                w = hi - lo
                act.wait_ge(s_ps, u + 1)
                if u >= NGB:
                    act.wait_ge(g_used, (u - NGB) // 2 + 1)
                b = 2 * (u % SLOTS)
                nc.scalar.activation(g[:, u % NGB, :, 0:w], ps[0:TP, b:b + 2, 0:w], ACT.Square,
                                     bias=sc2_col[0:TP, :]).then_inc(g_ready, 1)
            for t in range(T):
                act.wait_ge(var2_ready, t + 1)
                nc.scalar.activation(rstd[:, t:t + 1], rstd[:, t:t + 1], ACT.Sqrt).then_inc(std2_ready, 1)
            for t in range(T):
                act.wait_ge(x2T_ps, t + 1)
                nc.scalar.copy(x2nT[:, :, TP * t:TP * (t + 1)], x2T_bank(t)).then_inc(x2T_ready, 1)
            act.wait_ge(in_gate, 48)

            def hidden(again):
                for k in range(KH):
                    act.wait_ge(f_ps, again * KH + k + 1)
                    nc.scalar.activation(hT[:, k, :], psf[:, 1024 * (k % 2):1024 * (k % 2) + N], ACT.Gelu,
                                         bias=b1_sb[:, k:k + 1]).then_inc(h_ready, 1)

            hidden(0)
            act.wait_ge(ex_in, 1)
            nc.scalar.activation(ex[:, :, :], lg[:, :, :], ACT.Exp).then_inc(ex_ready, 1)
            for c in range(KC):
                act.wait_ge(xT_ps, KC + c + 1)
                nc.scalar.copy(x2nT[:, c, :], psf[:, 1024 * c:1024 * c + N]).then_inc(xT_ready, 1)
            hidden(1)

        @block.vector
        def _(dve):
            made = [0]

            def step(ins):
                made[0] += 1
                ins.then_inc(dve_chain, 1)
                dve.wait_ge(dve_chain, made[0])

            step(nc.vector.memset(sc2_col[:, :], SC2))
            dve.wait_ge(in_e, 32)
            nc.vector.tensor_copy(src_f[:, :], src_i[:, :])
            step(nc.vector.tensor_copy(dst_f[:, :], dst_i[:, :]))
            nc.vector.tensor_scalar(half_dst[:, :], dst_f[:, :], -1.0, 0.5, ALU.mult, ALU.add).then_inc(half_ready, 1)
            dve.wait_ge(pool_chain, 3)
            step(nc.vector.tensor_tensor(ge, dst_f[:, None, :].broadcast_to([TP, T + 1, NCH]),
                                         thr[:, :, None].broadcast_to([TP, T + 1, NCH]), ALU.is_ge))
            step(nc.vector.tensor_tensor(inr, ge[:, 0:T, :], ge[:, 1:T + 1, :], ALU.subtract))
            nc.vector.tensor_reduce(in_tile[:, :, :], inr.rearrange("p k (g j) -> p k g j", j=GC),
                                    AX.X, ALU.add).then_inc(flag_rows, 1)
            dve.wait_ge(in_x, 16)
            for t in range(T):
                step(nc.vector.bn_stats(bn[:, t, :], x_sb[:, t, :]))
                step(nc.vector.bn_aggr(mv[:, t, :], bn[:, t, :]))
            nc.vector.tensor_scalar(rstd[:, :], mv[:, :, 1], LN_EPS, None, ALU.add).then_inc(var_ready, 1)
            dve.wait_ge(flag_sum, 1)
            dve.wait_ge(pool_chain, 3 + T)
            step(nc.vector.tensor_scalar(flag_f[:, :, :], ps[0:1, 6, 0:T * NG].rearrange(
                "p (k g) -> p k g", k=T), 0.0, None, ALU.is_gt))
            step(nc.vector.tensor_tensor(flag_f[:, :, :], flag_f[:, :, :],
                                         bits[:, :, None].broadcast_to([1, T, NG]), ALU.mult))
            step(nc.vector.tensor_reduce(flag_g[:, :], flag_f[:, :, :].rearrange("p k g -> p g k"),
                                         AX.X, ALU.add))
            nc.vector.tensor_copy(flags[:, :], flag_g[:, :]).then_inc(flags_ready, 1)
            dve.wait_ge(std_ready, 1)
            step(nc.vector.reciprocal(rstd[:, :], rstd[:, :]))
            for t in range(T):
                ins = nc.vector.tensor_scalar(xn[:, t, :], x_sb[:, t, :], mv[:, t, 0:1], rstd[:, t:t + 1],
                                              ALU.subtract, ALU.mult)
            ins.then_inc(xn_ready, 1)
            def fill_chunk(b, j, col):
                ins = nc.vector.tensor_scalar(oh[:, b, 0, j, :], node_ids[:, :], src_f[:, bass.ds(col, 1)], None,
                                              ALU.is_equal)
                if j >= ACT_STEPS[b]:
                    ins = nc.vector.tensor_scalar(oh[:, b, 1, j, :], ids_m1[:, :], dst_f[:, bass.ds(col, 1)], 2.0,
                                                  ALU.is_ge, ALU.mult)
                if j == GC - 1:
                    ins.then_inc(oh_ready, 1)

            def fill(first, last):
                with dve.Fori(first, last) as i:
                    for b in range(2):
                        dve.wait_ge(oh_free, 2 * i + b + 1)
                        for j in range(GC):
                            fill_chunk(b, j, i * (2 * GC) + (b * GC + j))

            dve.wait_ge(in_bqkv, 16)
            dve.wait_ge(oh_free, 2)
            for t in range(T):
                dve.wait_ge(qkv_ps, t + 1)
                nc.vector.tensor_tensor(qk[:, t, :], ps[0:TP, 6 + t % 2, :], bqkv_sb[:, 0:2 * C], ALU.add)
                dve.wait_ge(z_copied, t + 1)
                nc.vector.tensor_tensor(v[:, t, :], ps[0:TP, 4 + t % 2, 0:C], bqkv_sb[:, 2 * C:3 * C], ALU.add
                                        ).then_inc(qkv_copied, 1)
                for n in range(2 * GC * t // T, 2 * GC * (t + 1) // T):
                    fill_chunk(n // GC, n % GC, n)
            dve.wait_ge(sq_ready, T)
            for w in range(2):
                ins = nc.vector.tensor_reduce(
                    nrm[:, w, :, :], sq[:, :, w * C:(w + 1) * C].rearrange("p t (h d) -> p t h d", d=D),
                    AX.X, ALU.add)
            ins.then_inc(norm_sq, 1)
            fill(1, 2)
            dve.wait_ge(norm_sd, 1)
            step(nc.vector.tensor_scalar(nrm[:, :, :, :], nrm[:, :, :, :], NORM_EPS, None, ALU.max))
            step(nc.vector.reciprocal(nrm[:, :, :, :], nrm[:, :, :, :]))
            dve.wait_ge(in_bias, 48)
            nc.vector.scalar_tensor_tensor(nrm[:, 0, :, :], nrm[:, 0, :, :], SC2,
                                           temp_sb[:, None, :].broadcast_to([TP, T, H]), ALU.mult, ALU.mult)
            nc.vector.tensor_scalar(nrm[:, 1, :, :], nrm[:, 1, :, :], SC, None, ALU.mult).then_inc(scales_ready, 1)
            fill(2, NG // 2)
            for n, (counts, sums) in enumerate(count_parts()):
                dve.wait_ge(A_left, n + 1)
                nc.vector.tensor_tensor(counts, sums[..., 1:AW], counts, ALU.subtract).then_inc(A_copied, 1)
            dve.wait_ge(m_ps, 1)
            for hg in range(2):
                nc.vector.tensor_tensor(MA[:, hg, :], ps[:, 4 + hg, 0:P], blk[:, :], ALU.mult)
                nc.vector.tensor_scalar(ks[:, hg:hg + 1], ps[:, 4 + hg, P:P + 1], 2 * SC2, None, ALU.mult)
                ins = nc.vector.tensor_scalar(vs[:, hg:hg + 1], ps[:, 4 + hg, P + 1:P + 2], SC2 * SC2, None, ALU.mult)
            ins.then_inc(m_ready, 1)
            dve.wait_ge(m_ready, 1)
            for n in range(1, 2 * H, 2):
                dve.wait_ge(st_ps, n + 1)
                nc.vector.tensor_copy(tiles(st[:, n % 2, n // 2, :]), wide_h(ST_BANKS[n % 4])).then_inc(st_copied_v, 1)
            for hg in range(2):
                dve.wait_ge(u_ps, hg + 1)
                nc.vector.scalar_tensor_tensor(uq[:, hg, :], psf[:, 1024 * hg:1024 * hg + N],
                                               ks[:, hg:hg + 1], qT[:, hg, :], ALU.add, ALU.mult
                                               ).then_inc(u_ready, 1)
            for hg in range(2):
                dve.wait_ge(n_ps, hg + 1)
                nc.vector.tensor_scalar(rn[:, hg, :], psf[:, 1024 * hg:1024 * hg + N],
                                        2.0 * N * SC2 * SC2, None, ALU.add).then_inc(n_ready, 1)
            dve.wait_ge(n_ready, 2)
            for hg in range(2):
                step(nc.vector.reciprocal(rn[:, hg, :], rn[:, hg, :]))
            for k in range(4):
                hg, (lo, hi) = k // 2, HALF[k % 2]
                dve.wait_ge(g_used, T * (k + 1))
                nc.vector.scalar_tensor_tensor(yT[:, hg, lo:hi], ps[:, 6 + k % 2, 0:hi - lo], vs[:, hg:hg + 1],
                                               rn[:, hg, lo:hi], ALU.add, ALU.mult).then_inc(y_ready, 1)
            dve.wait_ge(xb_ready, 1)
            for t in range(T + 1):
                if t < T:
                    dve.wait_ge(rp_ps, t + 1)
                    a = ps[0:TP, 2 * (t % 2), :]
                    rest = ps[0:TP, 2 * (t % 2) + 1, :]
                    step(nc.vector.tensor_scalar(cnt[:, t:t + 1], a[:, C:C + 1], 2.0, None, ALU.max))
                    step(nc.vector.reciprocal(cnt[:, t:t + 1], cnt[:, t:t + 1]))
                    step(nc.vector.scalar_tensor_tensor(x2[:, t, :], a[:, 0:C], cnt[:, t:t + 1], xb[:, t, :],
                                                        ALU.mult, ALU.add))
                    nc.vector.tensor_tensor(x2[:, t, :], x2[:, t, :], rest[:, 0:C], ALU.add).then_inc(x2_ready, 1)
                    dve.wait_ge(x2_ready, t + 1)
                    step(nc.vector.bn_stats(bn[:, t, :], x2[:, t, :]))
                    step(nc.vector.bn_aggr(mv[:, t, :], bn[:, t, :]))
                    nc.vector.tensor_scalar(rstd[:, t:t + 1], mv[:, t, 1:2], LN_EPS, None, ALU.add
                                            ).then_inc(var2_ready, 1)
                if t >= 1:
                    dve.wait_ge(std2_ready, t)
                    step(nc.vector.reciprocal(rstd[:, t - 1:t], rstd[:, t - 1:t]))
                    nc.vector.tensor_scalar(x2n[:, t - 1, :], x2[:, t - 1, :], mv[:, t - 1, 0:1], rstd[:, t - 1:t],
                                            ALU.subtract, ALU.mult).then_inc(xn2_ready, 1)
            dve.wait_ge(xn2_ready, T)
            step(nc.vector.tensor_copy(xs[:, 0], x2n))
            step(nc.vector.tensor_tensor(v[:, :, :], x2n, xs[:, 0], ALU.subtract))
            step(nc.vector.tensor_copy(xs[:, 1], v[:, :, :]))
            step(nc.vector.tensor_tensor(v[:, :, :], v[:, :, :], xs[:, 1], ALU.subtract))
            nc.vector.tensor_copy(xs[:, 2], v[:, :, :]).then_inc(xs_ready, 1)
            dve.wait_ge(lg_ps, 1)
            dve.wait_ge(in_gate, 48)
            step(nc.vector.tensor_tensor(lg[:, :, :], ps[0:TP, 4, 0:T * E].rearrange("p (t e) -> p t e", e=E),
                                         bg_sb[:, None, :].broadcast_to([TP, T, E]), ALU.add))
            step(nc.vector.tensor_reduce(mx[:, :], lg[:, :, :], AX.X, ALU.max))
            mxb = mx[:, :, None].broadcast_to([TP, T, E])
            nc.vector.tensor_tensor(lg[:, :, :], lg[:, :, :], mxb, ALU.subtract).then_inc(ex_in, 1)
            dve.wait_ge(ex_in, 1)
            step(nc.vector.scalar_tensor_tensor(eq[:, :, :], lg[:, :, :], 0.0,
                                                erank[:, None, :].broadcast_to([TP, T, E]),
                                                ALU.is_equal, ALU.mult))
            step(nc.vector.tensor_reduce(rk[:, :], eq[:, :, :], AX.X, ALU.max))
            nc.vector.tensor_tensor(eq[:, :, :], eq[:, :, :], rk[:, :, None].broadcast_to([TP, T, E]),
                                    ALU.is_equal).then_inc(rank_in, 1)
            dve.wait_ge(rank_in, 1)
            dve.wait_ge(ex_ready, 1)
            step(nc.vector.tensor_reduce(se[:, :], ex[:, :, :], AX.X, ALU.add))
            step(nc.vector.reciprocal(se[:, :], se[:, :]))
            nc.vector.tensor_tensor(selp, eq[:, :, :], se[:, :, None].broadcast_to([TP, T, E]), ALU.mult)
            dve.wait_ge(rank_ps, 1)
            pre = ps[0:TP, 5, 0:T * E].rearrange("p (t e) -> p e t", e=E)
            step(nc.vector.tensor_copy(tot[:, :, :], ps[0:TP, 6, 0:T * E].rearrange("p (t e) -> p e t", e=E)))
            flat = [a[:, :, :].rearrange("p e t -> p (e t)") for a in (tot, inc)]
            step(nc.vector.tensor_tensor_scan(flat[1], ones_c[0:TP, 0:T * E], flat[0], 0.0, ALU.mult, ALU.add))
            step(nc.vector.tensor_tensor(at_e[:, :, :], inc[:, :, :], tot[:, :, :], ALU.subtract))
            step(nc.vector.tensor_tensor(at_e[:, :, :], at_e[:, :, :], pre, ALU.add))
            step(nc.vector.tensor_tensor(at_e[:, :, :], at_e[:, :, :], eq[:, :, :].rearrange("p t e -> p e t"),
                                         ALU.mult))
            step(nc.vector.tensor_reduce(pos_f[:, :], at_e[:, :, :].rearrange("p e t -> p t e"), AX.X, ALU.add))
            nc.vector.tensor_copy(pos[:, :], pos_f[:, :]).then_inc(pos_ready, 1)
            for t in range(T):
                nc.vector.tensor_scalar(perm[:, t, :], node_ids[:, 0:PW], pos_f[:, t:t + 1], None, ALU.is_equal
                                        ).then_inc(perm_ready, 1)
            dve.wait_ge(rows_back, 16)
            nc.vector.tensor_copy(node_u[:, :], node)
            dve.wait_ge(esum_ps, 1)
            step(nc.vector.tensor_scalar(eflag_f[:, :, :], ps[0:1, 4, 64:64 + T * E].rearrange(
                "p (t e) -> p t e", e=E), 0.0, None, ALU.is_gt))
            step(nc.vector.tensor_tensor(eflag_f[:, :, :], eflag_f[:, :, :],
                                         bits[:, :, None].broadcast_to([1, T, E]), ALU.mult))
            step(nc.vector.tensor_reduce(eflag_g[:, :], eflag_f[:, :, :].rearrange("p t e -> p e t"),
                                         AX.X, ALU.add))
            nc.vector.tensor_copy(eflags[:, :], eflag_g[:, :]).then_inc(eflags_ready, 1)
            dve.wait_ge(selT_ps, 1)
            nc.vector.tensor_copy(tiles(selT[:, :]), wide(5)[0:E]).then_inc(selT_ready, 1)
            for t in range(T):
                dve.wait_ge(bd_ps, t + 1)
                nc.vector.tensor_tensor(x2[:, t, :], x2[:, t, :], ps[0:TP, t, 0:C], ALU.add
                                        ).then_inc(acc_ready, 1)
            with dve.Fori(0, E) as e:
                for t in range(T):
                    dve.wait_ge(e_ps, e * T + (t + 1))
                    dve.wait_ge(acc_ready, e * T + (t + 1))
                    nc.vector.scalar_tensor_tensor(x2[:, t, :], ps[0:TP, t, 0:C],
                                                   row[:, t, bass.ds(e + 2 * C, 1)], x2[:, t, :],
                                                   ALU.mult, ALU.add).then_inc(acc_ready, 1)
        @block.tensor
        def _(pe):
            mm = nc.tensor.matmul
            pe.sem_inc(oh_free, 2)
            pe.wait_ge(pool_const, 1)
            pe.wait_ge(flag_rows, 1)
            mm(ps[0:1, 6, 0:T * NG], ones_c[0:TP, 0:1], in_tile[:, :, :].rearrange("p k g -> p (k g)"),
               start=True, stop=True).then_inc(flag_sum, 1)

            pe.wait_ge(xn_ready, 1)
            for c in range(KC):
                for t in range(T):
                    ins = nc.tensor.transpose(wide(2 * c)[:, t, :], xn[:, t, P * c:P * (c + 1)], ident[0:TP, 0:TP])
                ins.then_inc(xT_ps, 1)
            pe.wait_ge(in_wqkv, 16)
            pe.wait_ge(in_wlr, 16)
            pe.wait_ge(xT_ready, KC)
            for t in range(T):
                if t >= 2:
                    pe.wait_ge(qkv_copied, t - 1)
                    pe.wait_ge(z_copied, t - 1)
                own = slice(TP * t, TP * (t + 1))
                for lo, hi, b, w in ((0, 2 * C, 6 + t % 2, wqkv_sb[:, :, 0:2 * C]),
                                     (0, C, 4 + t % 2, wqkv_sb[:, :, 2 * C:3 * C]),
                                     (C, 2 * C, 4 + t % 2, wlr_sb[:, :, 0:C])):
                    for c in range(KC):
                        ins = mm(ps[0:TP, b, lo:hi], xnT[:, c, own], w[:, c, :], start=(c == 0), stop=(c == KC - 1))
                ins.then_inc(qkv_ps, 1)
            pe.wait_ge(qkv_copied, T)
            pe.wait_ge(z_copied, T)
            pe.wait_ge(flags_ready, 1)
            for b in range(7):
                mm(ps[:, b, :], zeros[:, 0:P], zeros[:, :], start=True, stop=False, skip_group_check=True)
            with pe.Fori(0, NG // 2) as i:
                for b in range(2):
                    has = pe.value_load(flags[0:1, bass.ds(i * 2 + b, 1)])
                    pe.wait_ge(oh_ready, 2 * i + b + 1)
                    pe.wait_ge(steps_ready, 2 * i + b + 1)
                    for t in range(T):
                        with pe.If((has & (1 << t)) != 0):
                            for j in range(GC):
                                for s in range(T):
                                    mm(a_block(s, t), oh[:, b, 0, j, TP * s:TP * s + P],
                                       oh[:, b, 1, j, TP * t:TP * (t + 1) + 1], start=False, stop=False,
                                       skip_group_check=True)
                    mm(ps[:, 6, 256:384], zeros[:, 0:P], zeros[:, 0:P], start=False, stop=False,
                       skip_group_check=True).then_inc(oh_free, 1)
            for b in range(7):
                ins = mm(ps[:, b, 0:2], zeros[:, 0:P], zeros[:, 0:2], start=False, stop=True, skip_group_check=True)
            ins.then_inc(A_done, 1)
            pe.wait_ge(hl_ready, T)
            for c in range(2):
                pe.wait_ge(A_copied, 2 * c + 2)
                for t in range(T):
                    ins = nc.tensor.transpose(wide(2 * c)[:, t, :], qk[:, t, P * c:P * (c + 1)], ident[0:TP, 0:TP])
                ins.then_inc(qkT_ps, 1)
            pe.wait_ge(pool_const, 2)
            pe.wait_ge(A_copied, T + 2)
            for hg in range(2):
                k_h = slice(C + P * hg, C + P * (hg + 1))
                for t in range(T):
                    mm(ps[:, 4 + hg, 0:P], qk[:, t, k_h], qk[:, t, k_h], start=(t == 0), stop=(t == T - 1))
                for t in range(T):
                    mm(ps[:, 4 + hg, P:P + 1], qk[:, t, k_h], ones_c[0:TP, 0:1], start=(t == 0), stop=(t == T - 1))
                for t in range(T):
                    ins = mm(ps[:, 4 + hg, P + 1:P + 2], v[:, t, P * hg:P * (hg + 1)], ones_c[0:TP, 0:1],
                             start=(t == 0), stop=(t == T - 1))
            ins.then_inc(m_ps, 1)
            for n in range(2 * H):
                h, w = n // 2, n % 2
                if n == 2:
                    pe.wait_ge(m_ready, 1)
                if n >= 4:
                    pe.wait_ge(st_copied_v if n % 2 else st_copied_a, (n - 4) // 2 + 1)
                for t in range(T):
                    parts = [(0, 0, 2 * D), (2 * D, D, 2 * D), (3 * D, 0, D)] if w else [(0, 0, 2 * D), (2 * D, 0, 2 * D)]
                    both = hl[:, t, w, h].rearrange("p i d -> p (i d)")
                    for at, lo, hi in parts:
                        ins = nc.tensor.transpose(wide_h(ST_BANKS[n % 4])[at:at + hi - lo, t, :], both[:, lo:hi],
                                                  identh[0:TP, 0:TP])
                ins.then_inc(st_ps, 1)
            pe.wait_ge(qkT_copied, 2)
            for hg in range(2):
                for lo, hi in SPLIT:
                    ins = mm(psf[:, 1024 * hg + lo:1024 * hg + hi], MA[:, hg, :], qT[:, hg, lo:hi],
                             start=True, stop=True)
                ins.then_inc(u_ps, 1)
            for hg in range(2):
                pe.wait_ge(u_ready, hg + 1)
                for lo, hi in SPLIT:
                    ins = mm(psf[:, 1024 * hg + lo:1024 * hg + hi], blk[:, :], uq[:, hg, lo:hi],
                             start=True, stop=True)
                ins.then_inc(n_ps, 1)
            pe.wait_ge(n_ready, 2)
            pe.wait_ge(st_copied_a, H)
            pe.wait_ge(st_copied_v, H)

            def scores(u):
                hg, hf, m, pr = units[u]
                lo, hi = HALF[hf]
                if u >= SLOTS:
                    pe.wait_ge(g_ready, u - SLOTS + 1)
                for i in range(2):
                    h = HG * hg + 2 * pr + i
                    ins = mm(ps[0:TP, 2 * (u % SLOTS) + i, 0:hi - lo], st[:, 1, h, TP * m:TP * (m + 1)],
                             st[:, 0, h, lo:hi], start=True, stop=True)
                ins.then_inc(s_ps, 1)

            def values(u2):
                hg, hf, m, _ = units[2 * u2]
                lo, hi = HALF[hf]
                k = 2 * hg + hf
                pe.wait_ge(g_ready, 2 * u2 + 2)
                if m == 0 and k >= 2:
                    pe.wait_ge(y_ready, k - 1)
                for pr in range(2):
                    for i in range(2):
                        h = 2 * pr + i
                        ins = mm(ps[D * h:D * (h + 1), 6 + k % 2, 0:hi - lo],
                                 v[:, m, P * hg + D * h:P * hg + D * (h + 1)],
                                 g[:, (2 * u2 + pr) % NGB, i, 0:hi - lo], start=(m == 0), stop=(m == T - 1),
                                 tile_position=(0, D * h), skip_group_check=True)
                ins.then_inc(g_used, 1)

            U2 = len(units) // 2
            scores(0)
            scores(1)
            for u2 in range(U2):
                if u2 + 1 < U2:
                    scores(2 * u2 + 2)
                    scores(2 * u2 + 3)
                values(u2)
            pe.wait_ge(g_ready, len(units))
            pe.wait_ge(y_ready, 4)
            pe.wait_ge(in_wproj, 16)
            for t in range(T):
                if t >= 2:
                    pe.wait_ge(x2_ready, t - 1)
                own = slice(TP * t, TP * (t + 1))
                b = 2 * (t % 2)
                for s in range(T):
                    mm(ps[0:TP, b, 0:C + 1], AT[:, s, own], z[:, s, :], start=(s == 0), stop=(s == T - 1))
                for c in range(KC):
                    mm(ps[0:TP, b + 1, 0:C], xnT[:, c, own], wlr_sb[:, c, C:2 * C], start=(c == 0), stop=False)
                for c in range(KC):
                    ins = mm(ps[0:TP, b + 1, 0:C], yT[:, c, own], wproj_sb[:, c, :], start=False,
                             stop=(c == KC - 1))
                ins.then_inc(rp_ps, 1)
            for t in range(T):
                pe.wait_ge(xn2_ready, t + 1)
                if t >= 4:
                    pe.wait_ge(x2T_ready, t - 3)
                for c in range(KC):
                    ins = nc.tensor.transpose(x2T_bank(t)[:, c], x2n[:, t, P * c:P * (c + 1)], ident[0:TP, 0:TP])
                ins.then_inc(x2T_ps, 1)

            def hidden(again):
                for k in range(KH):
                    if k >= 2:
                        pe.wait_ge(h_ready, again * KH + k - 1)
                    if again and k == KH // 2:
                        pe.wait_ge(rows_back, 16)
                        for t in range(T):
                            ins = mm(ps[0:1, 4, 64 + E * t:64 + E * (t + 1)], ones_c[0:TP, 0:1], selp[:, t, :],
                                     start=True, stop=True)
                        ins.then_inc(esum_ps, 1)
                        for t in range(T):
                            ins = nc.tensor.transpose(wide(5)[0:E, t, :], selp[:, t, :], ident[0:TP, 0:TP])
                        ins.then_inc(selT_ps, 1)
                    for lo, hi in SPLIT:
                        for c in range(KC):
                            ins = mm(psf[:, 1024 * (k % 2) + lo:1024 * (k % 2) + hi],
                                     w1_sb[:, c, P * k:P * (k + 1)], x2nT[:, c, lo:hi],
                                     start=(c == 0), stop=(c == KC - 1))
                    ins.then_inc(f_ps, 1)

            pe.wait_ge(in_w1, 16)
            pe.wait_ge(x2T_ready, T)
            hidden(0)
            pe.wait_ge(in_gate, 48)
            pe.wait_ge(h_ready, KH)
            for t in range(T):
                for k in range(KH):
                    ins = mm(ps[0:TP, 4, E * t:E * (t + 1)], hT[:, k, TP * t:TP * (t + 1)], wg_sb[:, k, :],
                             start=(k == 0), stop=(k == KH - 1))
            ins.then_inc(lg_ps, 1)
            pe.wait_ge(rank_in, 1)
            sel = eq[:, :, :].rearrange("p t e -> p (t e)")
            mm(ps[0:TP, 5, 0:T * E], tri[:, :], sel, start=True, stop=True)
            mm(ps[0:TP, 6, 0:T * E], ones_c[0:TP, 0:TP], sel, start=True, stop=True).then_inc(rank_ps, 1)
            pe.wait_ge(xs_ready, 1)
            pe.wait_ge(perm_ready, T)
            for c in range(KC):
                for lo, hi in SPLIT:
                    for n in range(3 * T):
                        ins = mm(psf[:, 1024 * c + lo:1024 * c + hi], xs[:, n // T, n % T, P * c:P * (c + 1)],
                                 perm[:, n % T, lo:hi], start=(n == 0), stop=(n == 3 * T - 1))
                ins.then_inc(xT_ps, 1)
            pe.wait_ge(xT_ready, 2 * KC)
            hidden(1)
            pe.wait_ge(h_ready, 2 * KH)
            pe.wait_ge(selT_ready, 1)
            pe.wait_ge(in_bd, 16)
            for t in range(T):
                mm(ps[0:TP, t, 0:C], selT[:, TP * t:TP * (t + 1)], bd_sb[:, :],
                   start=True, stop=True).then_inc(bd_ps, 1)
            pe.wait_ge(in_wd, 16 * E)
            pe.wait_ge(eflags_ready, 1)
            with pe.Fori(0, E) as e:
                has = pe.value_load(eflags[0:1, bass.ds(e, 1)])
                for t in range(T):
                    pe.wait_ge(acc_ready, e * T + (t + 1))
                    with pe.If((has & (1 << t)) != 0):
                        for k in range(KH):
                            ins = mm(ps[0:TP, t, 0:C], hT[:, k, TP * t:TP * (t + 1)],
                                     wd_sb[:, bass.ds(e, 1), k, :], start=(k == 0), stop=(k == KH - 1))
                        ins.then_inc(e_ps, 1)
                    with pe.Else():
                        mm(ps[0:TP, t, 0:C], zeros[:, 0:TP], zeros[:, 0:C], start=True, stop=True).then_inc(e_ps, 1)


_OUT = (625, 256)


def kernel(**inputs):
    import numpy as np
    import concourse.bacc as bacc
    from concourse.bass_utils import run_bass_kernel_spmd

    a = {k: np.asarray(v) for k, v in inputs.items()}

    def rows(w, k):
        return np.ascontiguousarray(w.reshape(k, 128, -1).transpose(1, 0, 2))

    tp = 125
    arrays = {
        "x": np.ascontiguousarray(a["x"]),
        "src": np.ascontiguousarray(a["src"].reshape(-1, tp).T),
        "dst": np.ascontiguousarray(a["dst"].reshape(-1, tp).T),
        "w_qkv": rows(a["L0_mix_Wqkv"].T, 2),
        "b_qkv": a["L0_mix_bqkv"].reshape(1, -1),
        "w_lr": rows(np.concatenate([a["L0_gnn_W_l"].T, a["L0_gnn_W_r"].T], axis=1), 2),
        "b_r": a["L0_gnn_b_r"].reshape(1, -1),
        "w_proj": rows(a["L0_mix_Wproj"].T, 2),
        "b_proj": a["L0_mix_bproj"].reshape(1, -1),
        "temp": a["L0_mix_temperature"].reshape(1, -1),
        "w1": rows(a["L0_ffn_W1"], 2),
        "b1": np.ascontiguousarray(a["L0_ffn_b1"].reshape(8, 128).T),
        "wg": rows(a["L0_ffn_Wg"], 8),
        "bg": a["L0_ffn_bg"].reshape(1, -1),
        "wd": np.ascontiguousarray(a["L0_ffn_Wd"].reshape(8, 8, 128, 256).transpose(2, 0, 1, 3)),
        "bd": np.ascontiguousarray(a["L0_ffn_bd"]),
    }
    nc = bacc.Bacc("TRN2", target_bir_lowering=False, num_devices=1)
    args = [nc.dram_tensor(f"in_{n}", v.shape, mybir.dt.from_np(v.dtype), kind="ExternalInput").ap()
            for n, v in arrays.items()]
    out = nc.dram_tensor("out_0", _OUT, F32, kind="ExternalOutput").ap()
    rows_sorted = nc.dram_tensor("rows_sorted", (625, 521), F32, kind="Internal").ap()
    gps_layer(nc, *args, rows_sorted, out)
    r = run_bass_kernel_spmd(nc, [{f"in_{n}": v for n, v in arrays.items()}], core_ids=[0])
    return r.results[0]["out_0"]
```

```python
from contextlib import ExitStack

import concourse.bass as bass
from concourse import mybir

F32 = mybir.dt.float32
F16 = mybir.dt.float16
BF16 = mybir.dt.bfloat16
I32 = mybir.dt.int32
U32 = mybir.dt.uint32
ALU = mybir.AluOpType
ACT = mybir.ActivationFunctionType
AX = mybir.AxisListType

P = 128
LN_EPS = 1e-5
NORM_EPS = 1e-12


def gps_layer(nc, x, src, dst, w_qkv, b_qkv, w_lr, b_r, w_proj, b_proj, temp,
              w1, b1, wg, bg, wd, bd, rows_sorted, out):
    N, C = x.shape
    TP = 125
    T = N // TP
    KC = C // P
    NCH = src.shape[1]
    GC = 10
    NG = NCH // GC
    OHW = TP * (T - 1) + P
    H = temp.shape[1]
    D = C // H
    HG = P // D
    SC2 = float(D) ** 0.5
    SC = SC2 ** 0.5
    HID = w1.shape[2]
    KH = HID // P
    E = bg.shape[1]
    HALF = [(0, (N + 1) // 2), ((N + 1) // 2, N)]
    HW = HALF[0][1]
    BANK = 512
    SPLIT = [(0, BANK), (BANK, N)]
    EB = 4
    assert (T + E - 1) % EB == 0 and EB <= T
    assert N == T * TP and NG * GC == NCH and NG % 2 == 0 and H == 2 * HG

    with ExitStack() as ctx:
        def sb(name, shape, dt=F32):
            return ctx.enter_context(nc.sbuf_tensor(name, shape, dt))

        def sem(name):
            return ctx.enter_context(nc.semaphore(name))

        ps = ctx.enter_context(nc.psum_tensor("ps", [P, 8, BANK], F32))
        psf = ps[:, :, :].rearrange("p b n -> p (b n)")

        x_sb = sb("x_sb", [TP, T, C])
        src_i = sb("src_i", [TP, NCH], I32)
        dst_i = sb("dst_i", [TP, NCH], I32)
        wqkv_sb = sb("wqkv_sb", [P, KC, 3 * C])
        bqkv_sb = sb("bqkv_sb", [TP, 3 * C])
        wlr_sb = sb("wlr_sb", [P, KC, 2 * C])
        wproj_sb = sb("wproj_sb", [P, KC, C])
        br_sb = sb("br_sb", [TP, C])
        bproj_sb = sb("bproj_sb", [TP, C])
        temp_sb = sb("temp_sb", [TP, H])
        w1_sb = sb("w1_sb", [P, KC, HID])
        b1_sb = sb("b1_sb", [P, KH])
        wg_sb = sb("wg_sb", [P, KH, D])
        part_sum = sb("part_sum", [P, E])
        bg_sb = sb("bg_sb", [TP, E])
        WD = E * KH * C
        OH = 2 * 2 * GC * OHW // 2
        BIG = 2 * KH * N
        LATE = -(-(OH - BIG) // (KH * C))
        mem = sb("mem", [P, WD + BIG])
        wd_sb = mem[:, 0:WD].rearrange("p (e k c) -> p e k c", e=E, k=KH)
        big = mem[:, WD:WD + BIG]
        bd_sb = sb("bd_sb", [E, C])
        ident = sb("ident", [P, P])
        blk = sb("blk", [P, P])
        identh = sb("identh", [P, P], F16)
        node_ids = sb("node_ids", [TP, OHW], F16)
        ids_m1 = sb("ids_m1", [TP, OHW], F16)
        ones_c = sb("ones_c", [P, P])
        sc2_col = sb("sc2_col", [P, 1])
        zeros = sb("zeros", [TP, BANK], BF16)
        thr = sb("thr", [TP, T + 1])
        bits = sb("bits", [1, T])
        erank = sb("erank", [TP, E])
        src_f = sb("src_f", [TP, NCH])
        dst_f = sb("dst_f", [TP, NCH])
        half_src = sb("half_src", [TP, NCH])
        in_tile = sb("in_tile", [TP, T, NG])
        flag_f = sb("flag_f", [1, T, NG])
        flag_g = sb("flag_g", [1, NG])
        flag_w = sb("flag_w", [1, T, NG])
        flag_m = sb("flag_m", [1, NG])
        flags = sb("flags", [1, NG], I32)
        at_sb = sb("at_sb", [P, T * N])
        qk_sb = sb("qk_sb", [P, 2560])
        oh = mem[0:TP, WD + BIG - OH:WD + BIG].bitcast(BF16).rearrange("p (b w j n) -> p b w j n", b=2, w=2, j=GC)
        ge = big[0:TP, 0:(T + 1) * NCH].rearrange("p (k n) -> p k n", k=T + 1)
        inr = big[0:TP, (T + 1) * NCH:(2 * T + 1) * NCH].rearrange("p (k n) -> p k n", k=T)
        hT = big[:, 0:KH * N].rearrange("p (k n) -> p k n", k=KH)
        hT_step = big[:, KH * N:KH * N + EB * KH * TP].rearrange("p (b k n) -> p b k n", b=EB, k=KH)
        st = big[:, 0:H * N].bitcast(F16).rearrange("p (w h n) -> p w h n", w=2, h=H)
        qT = big[:, H * N:(H + 2) * N].rearrange("p (k n) -> p k n", k=2)
        rn = big[:, (H + 2) * N:(H + 4) * N].rearrange("p (k n) -> p k n", k=2)
        RW = rows_sorted.shape[1]
        row = sb("row", [TP, T, RW])
        x2 = row[:, :, 0:C]
        x2n = row[:, :, C:2 * C]
        selp = row[:, :, 2 * C:2 * C + E]
        node = row[:, :, 2 * C + E]
        bn = sb("bn", [TP, T, 6])
        mv = sb("mv", [TP, T, 2])
        rstd = sb("rstd", [TP, T])
        xn = x2n
        xnT = sb("xnT", [P, KC, N])
        xb = sb("xb", [TP, T, C])
        qk = qk_sb[0:TP, :].rearrange("p (t c) -> p t c", t=T)
        sq = at_sb[0:TP, 0:T * 2 * C].rearrange("p (t c) -> p t c", t=T)
        hl = row[:, :, 0:2 * C].bitcast(F16).rearrange("p t (w h i d) -> p t w h i d", w=2, h=H, i=2)
        v = sb("v", [TP, T, C])
        z = sb("z", [TP, T, C + 1])
        nrm = sb("nrm", [TP, 2, T, H])
        MA = sb("MA", [P, 2, P])
        ks = sb("ks", [P, 2])
        vs = sb("vs", [P, 2])
        NGB = 4
        g = qk_sb[0:TP, 0:NGB * 2 * HW].rearrange("p (b i n) -> p b i n", b=NGB, i=2)
        yT_sb = sb("yT_sb", [P, T * 2 * (P + 1)])
        yT = yT_sb[:, 0:2 * N].rearrange("p (k n) -> p k n", k=2)
        uq = yT
        kx = yT_sb[0:TP, :].rearrange("p (t g n) -> p t g n", t=T, g=2)
        PW = N + N % 2
        lgT = yT_sb[:, 0:N]
        selT = yT_sb[0:E, N:2 * N]
        perm = at_sb[0:TP, 0:T * PW // 2].bitcast(BF16).rearrange("p (t n) -> p t n", t=T)
        xs = qk_sb[0:TP, 0:3 * T * C // 2].bitcast(BF16).rearrange("p (i t c) -> p i t c", i=3, t=T)
        A = at_sb[0:TP, :].rearrange("p (t n) -> p t n", t=T)
        AT = big[0:TP, 0:T * N].rearrange("p (s n) -> p s n", s=T)
        cnt = sb("cnt", [TP, T])
        x2nT = xnT
        lg = sb("lg", [TP, T, E])
        mx = sb("mx", [TP, T])
        ex = sb("ex", [TP, T, E])
        se = sb("se", [TP, T])
        eq = sb("eq", [TP, T, E])
        rk = sb("rk", [TP, T])
        tri = sb("tri", [TP, TP])
        tot = sb("tot", [TP, E, T])
        inc = sb("inc", [TP, E, T])
        at_e = sb("at_e", [TP, E, T])
        pos_f = sb("pos_f", [TP, T])
        pos = sb("pos", [TP, T], U32)
        node_u = sb("node_u", [TP, T], U32)
        STEPS = T + E - 1
        step_m = sb("step_m", [1, STEPS])
        past = sb("past", [1, E - 1, T - 1])
        end_at = sb("end_at", [1, E - 1])
        ended = sb("ended", [1, STEPS, E - 1])
        stair_e = sb("stair_e", [1, STEPS])
        stair_t = sb("stair_t", [1, STEPS])
        stair_f = sb("stair_f", [1, 4, STEPS])
        stair = sb("stair", [1, 4, STEPS], I32)

        in_e = sem("in_e")
        in_x = sem("in_x")
        in_wqkv = sem("in_wqkv")
        in_bqkv = sem("in_bqkv")
        in_wlr = sem("in_wlr")
        in_bias = sem("in_bias")
        in_wproj = sem("in_wproj")
        in_w1 = sem("in_w1")
        in_gate = sem("in_gate")
        in_wd = sem("in_wd")
        in_bd = sem("in_bd")
        pool_const = sem("pool_const")
        pool_chain = sem("pool_chain")
        dve_chain = sem("dve_chain")
        flag_rows = sem("flag_rows")
        flag_sum = sem("flag_sum")
        flags_ready = sem("flags_ready")
        oh_ready = sem("oh_ready")
        steps_ready = sem("steps_ready")
        half_ready = sem("half_ready")
        st_ps = sem("st_ps")
        wg_zero = sem("wg_zero")
        AT_ps = sem("AT_ps")
        AT_copied = sem("AT_copied")
        vs_ps = sem("vs_ps")
        lgT_ps = sem("lgT_ps")
        lgT_copied = sem("lgT_copied")
        z_copied = sem("z_copied")
        sq_ready = sem("sq_ready")
        var2_ready = sem("var2_ready")
        std2_ready = sem("std2_ready")
        xn2_ready = sem("xn2_ready")
        x2T_ps = sem("x2T_ps")
        x2T_ready = sem("x2T_ready")
        xs_ready = sem("xs_ready")
        perm_ready = sem("perm_ready")
        A_left = sem("A_left")
        st_copied_a = sem("st_copied_a")
        st_copied_v = sem("st_copied_v")
        hl_ready = sem("hl_ready")
        oh_free = sem("oh_free")
        var_ready = sem("var_ready")
        std_ready = sem("std_ready")
        xn_ready = sem("xn_ready")
        xT_ps = sem("xT_ps")
        xT_ready = sem("xT_ready")
        qkv_ps = sem("qkv_ps")
        qkv_copied = sem("qkv_copied")
        norm_sq = sem("norm_sq")
        norm_sd = sem("norm_sd")
        scales_ready = sem("scales_ready")
        qkT_ps = sem("qkT_ps")
        qkT_copied = sem("qkT_copied")
        A_done = sem("A_done")
        A_copied = sem("A_copied")
        xb_ready = sem("xb_ready")
        m_ps = sem("m_ps")
        m_ready = sem("m_ready")
        u_ps = sem("u_ps")
        u_ready = sem("u_ready")
        n_ps = sem("n_ps")
        n_ready = sem("n_ready")
        s_ps = sem("s_ps")
        g_ready = sem("g_ready")
        g_used = sem("g_used")
        y_ready = sem("y_ready")
        rp_ps = sem("rp_ps")
        x2_ready = sem("x2_ready")
        f_ps = sem("f_ps")
        h_ready = sem("h_ready")
        lg_ps = sem("lg_ps")
        ex_in = sem("ex_in")
        ex_ready = sem("ex_ready")
        rank_in = sem("rank_in")
        rank_ps = sem("rank_ps")
        pos_ready = sem("pos_ready")
        rows_sent = sem("rows_sent")
        rows_back = sem("rows_back")
        stair_ready = sem("stair_ready")
        hT_staged = sem("hT_staged")
        selT_ps = sem("selT_ps")
        selT_ready = sem("selT_ready")
        bd_ps = sem("bd_ps")
        acc_ready = sem("acc_ready")
        e_ps = sem("e_ps")
        out_sent = sem("out_sent")

        AW = TP + 1
        TW = (T - 1) * TP

        def a_last(t):
            return ps[:, 5 + t // 4, P * (t % 4):P * (t % 4) + AW]

        def count_parts():
            for t in range(T):
                yield A[:, t, 0:TW], ps[0:TP, t, 0:TW + 1]
            yield A[:, 0:4, TW:N], ps[0:TP, 5, :].rearrange("p (t n) -> p t n", n=P)[:, :, 0:AW]
            yield A[:, 4, TW:N], ps[0:TP, 6, 0:AW]

        def at_block(s, t):
            return ps[0:TP, s, TP * t:TP * (t + 1)] if t < 4 else ps[0:TP, 5 + s // 4, TP * (s % 4):TP * (s % 4 + 1)]

        def at_parts():
            for s in range(T):
                yield AT[:, s, 0:TW], ps[0:TP, s, 0:TW]
            yield AT[:, 0:4, TW:N], ps[0:TP, 5, 0:TW].rearrange("p (s n) -> p s n", n=TP)
            yield AT[:, 4, TW:N], ps[0:TP, 6, 0:TP]

        ACT_STEPS = (5, 6)

        def wide(b):
            return psf[:, BANK * b:BANK * b + T * P].rearrange("p (t n) -> p t n", n=P)[:, :, 0:TP]

        def wide_h(b):
            return ps[:, b, :].bitcast(F16)[:, 0:T * P].rearrange("p (t n) -> p t n", n=P)[:, :, 0:TP]

        def x2T_bank(t):
            return ps[:, 4 + t % 4, 0:KC * TP].rearrange("p (c n) -> p c n", c=KC)

        ST_BANKS = (6, 7, 4, 5)
        RP_BANKS = ((0, 7), (2, 1))

        def tiles(row):
            return row.rearrange("p (t n) -> p t n", n=TP)

        units = [(hg, hf, m, pr) for hg in range(2) for hf in range(2) for m in range(T) for pr in range(2)]
        SLOTS = 3

        block = ctx.enter_context(nc.Block())

        @block.sync
        def _(sp):
            sp.dma_start(src_i[:, :], src).then_inc(in_e, 16)
            sp.dma_start(dst_i[:, :], dst).then_inc(in_e, 16)
            sp.dma_start(wqkv_sb[:, :, :], w_qkv).then_inc(in_wqkv, 16)
            sp.dma_start(bqkv_sb[:, :], b_qkv.partition_broadcast(TP)).then_inc(in_bqkv, 16)
            sp.dma_start(wlr_sb[:, :, :], w_lr).then_inc(in_wlr, 16)
            sp.dma_start(br_sb[:, :], b_r.partition_broadcast(TP)).then_inc(in_bias, 16)
            sp.dma_start(bproj_sb[:, :], b_proj.partition_broadcast(TP)).then_inc(in_bias, 16)
            sp.dma_start(temp_sb[:, :], temp.partition_broadcast(TP)).then_inc(in_bias, 16)
            sp.dma_start(wproj_sb[:, :, :], w_proj).then_inc(in_wproj, 16)
            sp.dma_start(w1_sb[:, :, :], w1).then_inc(in_w1, 16)
            sp.dma_start(b1_sb[:, :], b1).then_inc(in_gate, 16)
            sp.wait_ge(wg_zero, 1)
            sp.dma_start(wg_sb[:, :, 0:E], wg).then_inc(in_gate, 16)
            sp.dma_start(bg_sb[:, :], bg.partition_broadcast(TP)).then_inc(in_gate, 16)
            sp.dma_start(bd_sb[:, :], bd).then_inc(in_bd, 16)
            for e in range(E):
                if e == E - LATE:
                    sp.wait_ge(A_done, 1)
                sp.dma_start(wd_sb[:, e, :, :], wd[:, e, :, :]).then_inc(in_wd, 16)
            sp.wait_ge(rows_sent, 16 * T)
            sp.dma_start(row[:, :, :], rows_sorted.rearrange("(t p) c -> p t c", p=TP)).then_inc(rows_back, 16)

        @block.gpsimd
        def _(pool):
            made = [0]

            def step(ins):
                made[0] += 1
                ins.then_inc(pool_chain, 1)
                pool.wait_ge(pool_chain, made[0])

            step(nc.gpsimd.iota(node_ids[:, :], pattern=[[1, OHW]], base=0, channel_multiplier=0,
                                allow_small_or_imprecise_dtypes=True))
            step(nc.gpsimd.iota(ids_m1[:, :], pattern=[[1, OHW]], base=-1, channel_multiplier=0,
                                allow_small_or_imprecise_dtypes=True))
            step(nc.gpsimd.iota(thr[:, :], pattern=[[TP, T + 1]], base=0, channel_multiplier=0,
                                allow_small_or_imprecise_dtypes=True))
            for t in range(T):
                step(nc.gpsimd.memset(bits[:, t:t + 1], float(8 * 2 ** t)))
            step(nc.gpsimd.memset(ones_c[:, :], 1.0))
            step(nc.gpsimd.memset(ident[:, :], 0.0))
            step(nc.gpsimd.affine_select(out=ident[:, :], in_=ident[:, :], compare_op=ALU.not_equal, fill=1.0,
                                         base=0, pattern=[[-1, P]], channel_multiplier=1))
            step(nc.gpsimd.tensor_copy(identh[:, :], ident[:, :]))
            nc.gpsimd.memset(zeros[:, :], 0.0).then_inc(pool_const, 1)
            step(nc.gpsimd.iota(erank[:, :], pattern=[[-1, E]], base=E, channel_multiplier=0,
                                allow_small_or_imprecise_dtypes=True))
            step(nc.gpsimd.iota(step_m[:, :], pattern=[[1, STEPS]], base=-E, channel_multiplier=0,
                                allow_small_or_imprecise_dtypes=True))
            b4 = blk[:, :].rearrange("p (j d) -> p j d", d=D)
            step(nc.gpsimd.memset(blk[:, :], 1.0))
            step(nc.gpsimd.affine_select(out=b4, in_=b4, compare_op=ALU.is_ge, fill=0.0,
                                         base=0, pattern=[[-D, HG], [0, D]], channel_multiplier=1))
            step(nc.gpsimd.affine_select(out=b4, in_=b4, compare_op=ALU.is_ge, fill=0.0,
                                         base=D - 1, pattern=[[D, HG], [0, D]], channel_multiplier=-1))
            step(nc.gpsimd.memset(tri[:, :], 1.0))
            step(nc.gpsimd.affine_select(out=tri[:, :], in_=tri[:, :], compare_op=ALU.is_gt, fill=0.0,
                                         base=0, pattern=[[1, TP]], channel_multiplier=-1))
            nc.gpsimd.memset(z[:, :, C:C + 1], 1.0).then_inc(pool_const, 1)
            pool.wait_ge(in_x, 16)
            pool.wait_ge(in_bias, 48)
            step(nc.gpsimd.tensor_tensor(br_sb[:, :], br_sb[:, :], bproj_sb[:, :], ALU.add))
            for t in range(T):
                ins = nc.gpsimd.tensor_tensor(xb[:, t, :], x_sb[:, t, :], br_sb[:, :], ALU.add)
            ins.then_inc(xb_ready, 1)
            nc.gpsimd.iota(node, pattern=[[TP, T]], base=0, channel_multiplier=1,
                           allow_small_or_imprecise_dtypes=True).then_inc(pool_const, 1)
            step(nc.gpsimd.memset(kx[:, :, :, P:P + 1], 1.0))
            pool.wait_ge(scales_ready, 1)
            for t in range(T):
                q4 = qk[:, t, :].rearrange("p (w h d) -> p w h d", w=2, d=D)
                k4 = [kx[:, t, hg, 0:P].rearrange("p (h d) -> p h d", d=D) for hg in range(2)]
                scale = [nrm[:, w, t, :, None].broadcast_to([TP, H, D]) for w in range(2)]
                ins = nc.gpsimd.tensor_tensor(q4[:, 0], q4[:, 0], scale[0], ALU.mult)
                for hg in range(2):
                    own = slice(HG * hg, HG * (hg + 1))
                    ins = nc.gpsimd.tensor_tensor(k4[hg], q4[:, 1, own], scale[1][:, own], ALU.mult)
                step(ins)
                parts = [(hl[:, t, 0, :, :, :], q4[:, 0])]
                parts += [(hl[:, t, 1, HG * hg:HG * (hg + 1), :, :], k4[hg]) for hg in range(2)]
                for halves, whole in parts:
                    step(nc.gpsimd.tensor_copy(halves[:, :, 0, :], whole))
                    ins = nc.gpsimd.tensor_tensor(halves[:, :, 1, :], whole, halves[:, :, 0, :], ALU.subtract)
                ins.then_inc(hl_ready, 1)
            pool.wait_ge(pool_const, 3)
            pool.wait_ge(pos_ready, 1)
            for t in range(T):
                nc.gpsimd.indirect_dma_start(rows_sorted, bass.IndirectOffsetOnAxis(pos[:, t:t + 1], 0),
                                             row[:, t, :], None).then_inc(rows_sent, 16)
            for t in range(T):
                pool.wait_ge(acc_ready, T + E + t)
                nc.gpsimd.indirect_dma_start(out, bass.IndirectOffsetOnAxis(node_u[:, t:t + 1], 0),
                                             x2[:, t, :], None).then_inc(out_sent, 16)
            pool.wait_ge(out_sent, 16 * T)

        @block.scalar
        def _(act):
            act.dma_start(x_sb[:, :, :], x.rearrange("(t p) c -> p t c", p=TP)).then_inc(in_x, 16)
            act.wait_ge(var_ready, 1)
            nc.scalar.activation(rstd[:, :], rstd[:, :], ACT.Sqrt).then_inc(std_ready, 1)
            for c in range(KC):
                act.wait_ge(xT_ps, c + 1)
                nc.scalar.copy(tiles(xnT[:, c, :]), wide(2 * c)).then_inc(xT_ready, 1)
            act.wait_ge(pool_const, 2)
            for t in range(T):
                act.wait_ge(qkv_ps, t + 1)
                nc.scalar.copy(z[:, t, 0:C], ps[0:TP, 4 + t % 2, C:2 * C]).then_inc(z_copied, 1)
                act.wait_ge(qkv_copied, t + 1)
                nc.scalar.activation(sq[:, t, :], qk[:, t, :], ACT.Square).then_inc(sq_ready, 1)
            act.wait_ge(half_ready, 1)

            def steps(first, last):
                with act.Fori(first, last) as i:
                    for b in range(2):
                        act.wait_ge(oh_free, 2 * i + b + 1)
                        for j in range(ACT_STEPS[b]):
                            col = i * (2 * GC) + (b * GC + j)
                            ins = nc.scalar.activation(oh[:, b, 0, j, :], ids_m1[:, :], ACT.Sign,
                                                       bias=half_src[:, bass.ds(col, 1)])
                        ins.then_inc(steps_ready, 1)

            steps(0, 1)
            act.wait_ge(norm_sq, 1)
            nc.scalar.activation(nrm[:, 0, :, :], nrm[:, 0, :, :], ACT.Sqrt, scale=SC2)
            nc.scalar.activation(nrm[:, 1, :, :], nrm[:, 1, :, :], ACT.Sqrt).then_inc(norm_sd, 1)
            steps(1, NG // 2)
            act.wait_ge(A_done, 1)
            for counts, sums in count_parts():
                nc.scalar.copy(counts, sums[..., 0:counts.shape[-1]]).then_inc(A_left, 1)
            for c in range(2):
                act.wait_ge(qkT_ps, c + 1)
                nc.scalar.copy(tiles(qT[:, c, :]), wide(2 * c)).then_inc(qkT_copied, 1)
            for n in range(0, 2 * H, 2):
                act.wait_ge(st_ps, n + 1)
                nc.scalar.copy(tiles(st[:, n % 2, n // 2, :]), wide_h(ST_BANKS[n % 4])).then_inc(st_copied_a, 1)
            for u, (hg, hf, m, pr) in enumerate(units):
                lo, hi = HALF[hf]
                w = hi - lo
                act.wait_ge(s_ps, u + 1)
                if u >= NGB:
                    act.wait_ge(g_used, (u - NGB) // 2 + 1)
                b = 2 * (u % SLOTS)
                nc.scalar.activation(g[:, u % NGB, :, 0:w], ps[0:TP, b:b + 2, 0:w], ACT.Square,
                                     bias=sc2_col[0:TP, :]).then_inc(g_ready, 1)
            for t in range(T):
                act.wait_ge(var2_ready, t + 1)
                nc.scalar.activation(rstd[:, t:t + 1], rstd[:, t:t + 1], ACT.Sqrt).then_inc(std2_ready, 1)
            for t in range(T):
                act.wait_ge(x2T_ps, t + 1)
                nc.scalar.copy(x2nT[:, :, TP * t:TP * (t + 1)], x2T_bank(t)).then_inc(x2T_ready, 1)
            act.wait_ge(in_gate, 48)

            def hidden(again):
                for k in range(KH):
                    act.wait_ge(f_ps, again * KH + k + 1)
                    nc.scalar.activation(hT[:, k, :], psf[:, 1024 * (k % 2):1024 * (k % 2) + N], ACT.Gelu,
                                         bias=b1_sb[:, k:k + 1]).then_inc(h_ready, 1)

            hidden(0)
            act.wait_ge(ex_in, 1)
            nc.scalar.activation(ex[:, :, :], lg[:, :, :], ACT.Exp).then_inc(ex_ready, 1)
            for c in range(KC):
                act.wait_ge(xT_ps, KC + c + 1)
                nc.scalar.copy(x2nT[:, c, :], psf[:, 1024 * c:1024 * c + N]).then_inc(xT_ready, 1)
            hidden(1)
            act.wait_ge(stair_ready, 1)
            act.wait_ge(h_ready, 2 * KH)
            with act.Fori(0, STEPS // EB) as i:
                for b in range(EB):
                    first = act.value_load(stair[0:1, 1, bass.ds(i * EB + b, 1)], max_val=(T - 1) * TP)
                    act.wait_ge(e_ps, i * EB + (b + 1))
                    nc.scalar.copy(hT_step[:, b, :, :], hT[:, :, bass.ds(first, TP)]).then_inc(hT_staged, 1)

        @block.vector
        def _(dve):
            made = [0]

            def step(ins):
                made[0] += 1
                ins.then_inc(dve_chain, 1)
                dve.wait_ge(dve_chain, made[0])

            step(nc.vector.memset(sc2_col[:, :], SC2))
            nc.vector.memset(wg_sb[:, :, :], 0.0).then_inc(wg_zero, 1)
            dve.wait_ge(in_e, 32)
            nc.vector.tensor_copy(src_f[:, :], src_i[:, :])
            step(nc.vector.tensor_copy(dst_f[:, :], dst_i[:, :]))
            nc.vector.tensor_scalar(half_src[:, :], src_f[:, :], -1.0, 0.5, ALU.mult, ALU.add).then_inc(half_ready, 1)
            dve.wait_ge(pool_chain, 3)
            step(nc.vector.tensor_tensor(ge, dst_f[:, None, :].broadcast_to([TP, T + 1, NCH]),
                                         thr[:, :, None].broadcast_to([TP, T + 1, NCH]), ALU.is_ge))
            step(nc.vector.tensor_tensor(inr, ge[:, 0:T, :], ge[:, 1:T + 1, :], ALU.subtract))
            nc.vector.tensor_reduce(in_tile[:, :, :], inr.rearrange("p k (g j) -> p k g j", j=GC),
                                    AX.X, ALU.add).then_inc(flag_rows, 1)
            dve.wait_ge(in_x, 16)
            for t in range(T):
                step(nc.vector.bn_stats(bn[:, t, :], x_sb[:, t, :]))
                step(nc.vector.bn_aggr(mv[:, t, :], bn[:, t, :]))
            nc.vector.tensor_scalar(rstd[:, :], mv[:, :, 1], LN_EPS, None, ALU.add).then_inc(var_ready, 1)
            dve.wait_ge(flag_sum, 1)
            dve.wait_ge(pool_chain, 3 + T)
            step(nc.vector.tensor_scalar(flag_f[:, :, :], ps[0:1, 6, 0:T * NG].rearrange(
                "p (k g) -> p k g", k=T), 0.0, None, ALU.is_gt))
            dve.wait_ge(std_ready, 1)
            step(nc.vector.reciprocal(rstd[:, :], rstd[:, :]))
            for t in range(T):
                ins = nc.vector.tensor_scalar(xn[:, t, :], x_sb[:, t, :], mv[:, t, 0:1], rstd[:, t:t + 1],
                                              ALU.subtract, ALU.mult)
            ins.then_inc(xn_ready, 1)
            dve.wait_ge(pool_chain, 8 + T)
            step(nc.vector.tensor_tensor(flag_w[:, :, :], flag_f[:, :, :],
                                         erank[0:1, 0:T, None].broadcast_to([1, T, NG]), ALU.mult))
            step(nc.vector.tensor_reduce(flag_m[:, :], flag_w[:, :, :].rearrange("p k g -> p g k"),
                                         AX.X, ALU.max))
            step(nc.vector.tensor_tensor(flag_w[:, :, :], flag_w[:, :, :],
                                         flag_m[:, None, :].broadcast_to([1, T, NG]), ALU.not_equal))
            step(nc.vector.tensor_tensor(flag_f[:, :, :], flag_f[:, :, :],
                                         bits[:, :, None].broadcast_to([1, T, NG]), ALU.mult))
            step(nc.vector.tensor_tensor(flag_f[:, :, :], flag_f[:, :, :], flag_w[:, :, :], ALU.mult))
            step(nc.vector.tensor_reduce(flag_g[:, :], flag_f[:, :, :].rearrange("p k g -> p g k"),
                                         AX.X, ALU.add))
            step(nc.vector.tensor_tensor(flag_g[:, :], flag_g[:, :], flag_m[:, :], ALU.subtract))
            nc.vector.tensor_scalar(flags[:, :], flag_g[:, :], float(E), None, ALU.add).then_inc(flags_ready, 1)
            def fill_chunk(b, j, col):
                ins = nc.vector.tensor_scalar(oh[:, b, 1, j, :], node_ids[:, :], dst_f[:, bass.ds(col, 1)], None,
                                              ALU.is_equal)
                if j >= ACT_STEPS[b]:
                    ins = nc.vector.tensor_scalar(oh[:, b, 0, j, :], ids_m1[:, :], src_f[:, bass.ds(col, 1)], 2.0,
                                                  ALU.is_ge, ALU.mult)
                if j == GC - 1:
                    ins.then_inc(oh_ready, 1)

            def fill(first, last):
                with dve.Fori(first, last) as i:
                    for b in range(2):
                        dve.wait_ge(oh_free, 2 * i + b + 1)
                        for j in range(GC):
                            fill_chunk(b, j, i * (2 * GC) + (b * GC + j))

            dve.wait_ge(in_bqkv, 16)
            dve.wait_ge(oh_free, 2)
            for t in range(T):
                dve.wait_ge(qkv_ps, t + 1)
                nc.vector.tensor_tensor(qk[:, t, :], ps[0:TP, 6 + t % 2, :], bqkv_sb[:, 0:2 * C], ALU.add)
                dve.wait_ge(z_copied, t + 1)
                nc.vector.tensor_tensor(v[:, t, :], ps[0:TP, 4 + t % 2, 0:C], bqkv_sb[:, 2 * C:3 * C], ALU.add
                                        ).then_inc(qkv_copied, 1)
                for n in range(2 * GC * t // T, 2 * GC * (t + 1) // T):
                    fill_chunk(n // GC, n % GC, n)
            dve.wait_ge(sq_ready, T)
            for w in range(2):
                ins = nc.vector.tensor_reduce(
                    nrm[:, w, :, :], sq[:, :, w * C:(w + 1) * C].rearrange("p t (h d) -> p t h d", d=D),
                    AX.X, ALU.add)
            ins.then_inc(norm_sq, 1)
            dve.wait_ge(vs_ps, 1)
            step(nc.vector.tensor_scalar(vs[:, :], ps[:, 7, 0:2], SC2 * SC2, None, ALU.mult))
            fill(1, 2)
            dve.wait_ge(norm_sd, 1)
            step(nc.vector.tensor_scalar(nrm[:, :, :, :], nrm[:, :, :, :], NORM_EPS, None, ALU.max))
            step(nc.vector.reciprocal(nrm[:, :, :, :], nrm[:, :, :, :]))
            dve.wait_ge(in_bias, 48)
            nc.vector.scalar_tensor_tensor(nrm[:, 0, :, :], nrm[:, 0, :, :], SC2,
                                           temp_sb[:, None, :].broadcast_to([TP, T, H]), ALU.mult, ALU.mult)
            nc.vector.tensor_scalar(nrm[:, 1, :, :], nrm[:, 1, :, :], SC, None, ALU.mult).then_inc(scales_ready, 1)
            fill(2, NG // 2)
            for n, (counts, sums) in enumerate(count_parts()):
                dve.wait_ge(A_left, n + 1)
                nc.vector.tensor_tensor(counts, sums[..., 1:counts.shape[-1] + 1], counts, ALU.subtract).then_inc(A_copied, 1)
            dve.wait_ge(m_ps, 1)
            for hg in range(2):
                nc.vector.tensor_tensor(MA[:, hg, :], ps[:, 4 + hg, 0:P], blk[:, :], ALU.mult)
                ins = nc.vector.tensor_scalar(ks[:, hg:hg + 1], ps[:, 4 + hg, P:P + 1], 2 * SC2, None, ALU.mult)
            ins.then_inc(m_ready, 1)
            dve.wait_ge(m_ready, 1)
            for n in range(1, 2 * H, 2):
                dve.wait_ge(st_ps, n + 1)
                nc.vector.tensor_copy(tiles(st[:, n % 2, n // 2, :]), wide_h(ST_BANKS[n % 4])).then_inc(st_copied_v, 1)
            for hg in range(2):
                dve.wait_ge(u_ps, hg + 1)
                nc.vector.scalar_tensor_tensor(uq[:, hg, :], psf[:, 1024 * hg:1024 * hg + N],
                                               ks[:, hg:hg + 1], qT[:, hg, :], ALU.add, ALU.mult
                                               ).then_inc(u_ready, 1)
            for hg in range(2):
                dve.wait_ge(n_ps, hg + 1)
                nc.vector.tensor_scalar(rn[:, hg, :], psf[:, 1024 * hg:1024 * hg + N],
                                        2.0 * N * SC2 * SC2, None, ALU.add).then_inc(n_ready, 1)
            dve.wait_ge(n_ready, 2)
            for hg in range(2):
                step(nc.vector.reciprocal(rn[:, hg, :], rn[:, hg, :]))
            for k in range(4):
                hg, (lo, hi) = k // 2, HALF[k % 2]
                dve.wait_ge(g_used, T * (k + 1))
                nc.vector.scalar_tensor_tensor(yT[:, hg, lo:hi], ps[:, 6 + k % 2, 0:hi - lo], vs[:, hg:hg + 1],
                                               rn[:, hg, lo:hi], ALU.add, ALU.mult).then_inc(y_ready, 1)
            for n, (counts, blocks) in enumerate(at_parts()):
                dve.wait_ge(AT_ps, min(n + 1, T))
                nc.vector.tensor_copy(counts, blocks).then_inc(AT_copied, 1)
            dve.wait_ge(xb_ready, 1)
            for t in range(T + 1):
                if t < T:
                    dve.wait_ge(rp_ps, t + 1)
                    a, rest = (ps[0:TP, b, :] for b in RP_BANKS[t % 2])
                    step(nc.vector.tensor_scalar(cnt[:, t:t + 1], a[:, C:C + 1], 2.0, None, ALU.max))
                    step(nc.vector.reciprocal(cnt[:, t:t + 1], cnt[:, t:t + 1]))
                    step(nc.vector.scalar_tensor_tensor(x2[:, t, :], a[:, 0:C], cnt[:, t:t + 1], xb[:, t, :],
                                                        ALU.mult, ALU.add))
                    nc.vector.tensor_tensor(x2[:, t, :], x2[:, t, :], rest[:, 0:C], ALU.add).then_inc(x2_ready, 1)
                    dve.wait_ge(x2_ready, t + 1)
                    step(nc.vector.bn_stats(bn[:, t, :], x2[:, t, :]))
                    step(nc.vector.bn_aggr(mv[:, t, :], bn[:, t, :]))
                    nc.vector.tensor_scalar(rstd[:, t:t + 1], mv[:, t, 1:2], LN_EPS, None, ALU.add
                                            ).then_inc(var2_ready, 1)
                if t >= 1:
                    dve.wait_ge(std2_ready, t)
                    step(nc.vector.reciprocal(rstd[:, t - 1:t], rstd[:, t - 1:t]))
                    nc.vector.tensor_scalar(x2n[:, t - 1, :], x2[:, t - 1, :], mv[:, t - 1, 0:1], rstd[:, t - 1:t],
                                            ALU.subtract, ALU.mult).then_inc(xn2_ready, 1)
            dve.wait_ge(xn2_ready, T)
            step(nc.vector.tensor_copy(xs[:, 0], x2n))
            step(nc.vector.tensor_tensor(v[:, :, :], x2n, xs[:, 0], ALU.subtract))
            step(nc.vector.tensor_copy(xs[:, 1], v[:, :, :]))
            step(nc.vector.tensor_tensor(v[:, :, :], v[:, :, :], xs[:, 1], ALU.subtract))
            nc.vector.tensor_copy(xs[:, 2], v[:, :, :]).then_inc(xs_ready, 1)
            step(nc.vector.tensor_reduce(part_sum[:, :], ident[:, :].rearrange("p (j d) -> p d j", d=D)[:, 0:E, :],
                                         AX.X, ALU.add))
            dve.wait_ge(lgT_ps, 1)
            nc.vector.tensor_copy(lgT, psf[:, 4 * BANK:4 * BANK + N]).then_inc(lgT_copied, 1)
            dve.wait_ge(lg_ps, 1)
            dve.wait_ge(in_gate, 48)
            step(nc.vector.tensor_tensor(lg[:, :, :], ps[0:TP, 4, 0:T * E].rearrange("p (t e) -> p t e", e=E),
                                         bg_sb[:, None, :].broadcast_to([TP, T, E]), ALU.add))
            step(nc.vector.tensor_reduce(mx[:, :], lg[:, :, :], AX.X, ALU.max))
            mxb = mx[:, :, None].broadcast_to([TP, T, E])
            nc.vector.tensor_tensor(lg[:, :, :], lg[:, :, :], mxb, ALU.subtract).then_inc(ex_in, 1)
            dve.wait_ge(ex_in, 1)
            step(nc.vector.scalar_tensor_tensor(eq[:, :, :], lg[:, :, :], 0.0,
                                                erank[:, None, :].broadcast_to([TP, T, E]),
                                                ALU.is_equal, ALU.mult))
            step(nc.vector.tensor_reduce(rk[:, :], eq[:, :, :], AX.X, ALU.max))
            nc.vector.tensor_tensor(eq[:, :, :], eq[:, :, :], rk[:, :, None].broadcast_to([TP, T, E]),
                                    ALU.is_equal).then_inc(rank_in, 1)
            dve.wait_ge(rank_in, 1)
            dve.wait_ge(ex_ready, 1)
            step(nc.vector.tensor_reduce(se[:, :], ex[:, :, :], AX.X, ALU.add))
            step(nc.vector.reciprocal(se[:, :], se[:, :]))
            nc.vector.tensor_tensor(selp, eq[:, :, :], se[:, :, None].broadcast_to([TP, T, E]), ALU.mult)
            dve.wait_ge(rank_ps, 1)
            pre = ps[0:TP, 5, 0:T * E].rearrange("p (t e) -> p e t", e=E)
            step(nc.vector.tensor_copy(tot[:, :, :], ps[0:TP, 6, 0:T * E].rearrange("p (t e) -> p e t", e=E)))
            flat = [a[:, :, :].rearrange("p e t -> p (e t)") for a in (tot, inc)]
            step(nc.vector.tensor_tensor_scan(flat[1], ones_c[0:TP, 0:T * E], flat[0], 0.0, ALU.mult, ALU.add))
            step(nc.vector.tensor_tensor(at_e[:, :, :], inc[:, :, :], tot[:, :, :], ALU.subtract))
            step(nc.vector.tensor_tensor(at_e[:, :, :], at_e[:, :, :], pre, ALU.add))
            step(nc.vector.tensor_tensor(at_e[:, :, :], at_e[:, :, :], eq[:, :, :].rearrange("p t e -> p e t"),
                                         ALU.mult))
            step(nc.vector.tensor_reduce(pos_f[:, :], at_e[:, :, :].rearrange("p e t -> p t e"), AX.X, ALU.add))
            nc.vector.tensor_copy(pos[:, :], pos_f[:, :]).then_inc(pos_ready, 1)
            for t in range(T):
                nc.vector.tensor_scalar(perm[:, t, :], node_ids[:, 0:PW], pos_f[:, t:t + 1], None, ALU.is_equal
                                        ).then_inc(perm_ready, 1)
            step(nc.vector.tensor_tensor(past[:, :, :], inc[0:1, 0:E - 1, T - 1:T].broadcast_to([1, E - 1, T - 1]),
                                         thr[0:1, None, 1:T].broadcast_to([1, E - 1, T - 1]), ALU.is_gt))
            step(nc.vector.tensor_reduce(end_at[:, :], past[:, :, :], AX.X, ALU.add))
            step(nc.vector.tensor_tensor(end_at[:, :], end_at[:, :], erank[0:1, 0:E - 1], ALU.subtract))
            step(nc.vector.tensor_tensor(ended[:, :, :], step_m[:, :, None].broadcast_to([1, STEPS, E - 1]),
                                         end_at[:, None, :].broadcast_to([1, STEPS, E - 1]), ALU.is_gt))
            step(nc.vector.tensor_reduce(stair_e[:, :], ended[:, :, :], AX.X, ALU.add))
            step(nc.vector.scalar_tensor_tensor(stair_t[:, :], step_m[:, :], float(E), stair_e[:, :],
                                                ALU.add, ALU.subtract))
            nc.vector.tensor_copy(stair_f[:, 0, :], stair_e[:, :])
            nc.vector.tensor_scalar(stair_f[:, 1, :], stair_t[:, :], float(TP), None, ALU.mult)
            step(nc.vector.tensor_scalar(stair_f[:, 2, :], stair_t[:, :], float(RW), None, ALU.mult))
            step(nc.vector.scalar_tensor_tensor(stair_f[:, 3, :], stair_f[:, 2, :], 2.0 * C, stair_e[:, :],
                                                ALU.add, ALU.add))
            nc.vector.tensor_copy(stair[:, :, :], stair_f[:, :, :]).then_inc(stair_ready, 1)
            dve.wait_ge(rows_back, 16)
            nc.vector.tensor_copy(node_u[:, :], node)
            dve.wait_ge(selT_ps, 1)
            nc.vector.tensor_copy(tiles(selT), wide(5)[0:E]).then_inc(selT_ready, 1)
            for t in range(T):
                dve.wait_ge(bd_ps, t + 1)
                nc.vector.tensor_tensor(x2[:, t, :], x2[:, t, :], ps[0:TP, t, 0:C], ALU.add
                                        ).then_inc(acc_ready, 1)
            rows_flat = row[:, :, :].rearrange("p t c -> p (t c)")
            dve.wait_ge(stair_ready, 1)
            with dve.Fori(0, STEPS // EB) as i:
                for b in range(EB):
                    at_row = dve.value_load(stair[0:1, 2, bass.ds(i * EB + b, 1)], max_val=(T - 1) * RW)
                    at_prob = dve.value_load(stair[0:1, 3, bass.ds(i * EB + b, 1)], max_val=T * RW - 1)
                    tile_x2 = rows_flat[:, bass.ds(at_row, C)]
                    dve.wait_ge(e_ps, i * EB + (EB + b + 1))
                    dve.wait_ge(acc_ready, i * EB + (T + b))
                    nc.vector.scalar_tensor_tensor(tile_x2, ps[0:TP, b, 0:C], rows_flat[:, bass.ds(at_prob, 1)],
                                                   tile_x2, ALU.mult, ALU.add).then_inc(acc_ready, 1)

        @block.tensor
        def _(pe):
            mm = nc.tensor.matmul
            pe.sem_inc(oh_free, 2)
            pe.wait_ge(pool_const, 1)
            pe.wait_ge(flag_rows, 1)
            mm(ps[0:1, 6, 0:T * NG], ones_c[0:TP, 0:1], in_tile[:, :, :].rearrange("p k g -> p (k g)"),
               start=True, stop=True).then_inc(flag_sum, 1)

            pe.wait_ge(xn_ready, 1)
            for c in range(KC):
                for t in range(T):
                    ins = nc.tensor.transpose(wide(2 * c)[:, t, :], xn[:, t, P * c:P * (c + 1)], ident[0:TP, 0:TP])
                ins.then_inc(xT_ps, 1)
            pe.wait_ge(in_wqkv, 16)
            pe.wait_ge(in_wlr, 16)
            pe.wait_ge(xT_ready, KC)
            for t in range(T):
                if t >= 2:
                    pe.wait_ge(qkv_copied, t - 1)
                    pe.wait_ge(z_copied, t - 1)
                own = slice(TP * t, TP * (t + 1))
                for lo, hi, b, w in ((0, 2 * C, 6 + t % 2, wqkv_sb[:, :, 0:2 * C]),
                                     (0, C, 4 + t % 2, wqkv_sb[:, :, 2 * C:3 * C]),
                                     (C, 2 * C, 4 + t % 2, wlr_sb[:, :, 0:C])):
                    for c in range(KC):
                        ins = mm(ps[0:TP, b, lo:hi], xnT[:, c, own], w[:, c, :], start=(c == 0), stop=(c == KC - 1))
                ins.then_inc(qkv_ps, 1)
            pe.wait_ge(qkv_copied, T)
            pe.wait_ge(z_copied, T)
            for hg in range(2):
                for t in range(T):
                    ins = mm(ps[:, 7, hg:hg + 1], v[:, t, P * hg:P * (hg + 1)], ones_c[0:TP, 0:1],
                             start=(t == 0), stop=(t == T - 1))
            ins.then_inc(vs_ps, 1)
            pe.wait_ge(flags_ready, 1)
            for b in range(7):
                mm(ps[:, b, :], zeros[:, 0:P], zeros[:, :], start=True, stop=False, skip_group_check=True)
            with pe.Fori(0, NG // 2) as i:
                for b in range(2):
                    code = pe.value_load(flags[0:1, bass.ds(i * 2 + b, 1)], min_val=0, max_val=8 * 2 ** T - 1)
                    first = nc.s_assert_within(code & 7, min_val=0, max_val=T - 1,
                                               skip_runtime_bounds_check_because="each group has edges, each of a tile")
                    pe.wait_ge(oh_ready, 2 * i + b + 1)
                    pe.wait_ge(steps_ready, 2 * i + b + 1)
                    for j in range(GC):
                        node_of = oh[:, b, 1, j, bass.ds(first * TP, P)]
                        mm(psf[:, bass.ds(first * BANK, TW + 1)], node_of, oh[:, b, 0, j, 0:TW + 1],
                           start=False, stop=False, skip_group_check=True)
                        mm(psf[:, bass.ds(first * P + 5 * BANK, AW)], node_of, oh[:, b, 0, j, TW:N + 1],
                           start=False, stop=False, skip_group_check=True)
                    with pe.If(code > 7):
                        for t in range(1, T):
                            with pe.If((code & (8 << t)) != 0):
                                for j in range(GC):
                                    node_of = oh[:, b, 1, j, TP * t:TP * t + P]
                                    mm(ps[:, t, 0:TW + 1], node_of, oh[:, b, 0, j, 0:TW + 1],
                                       start=False, stop=False, skip_group_check=True)
                                    mm(a_last(t), node_of, oh[:, b, 0, j, TW:N + 1],
                                       start=False, stop=False, skip_group_check=True)
                    mm(ps[:, 6, 256:384], zeros[:, 0:P], zeros[:, 0:P], start=False, stop=False,
                       skip_group_check=True).then_inc(oh_free, 1)
            for b in range(7):
                ins = mm(ps[:, b, 0:2], zeros[:, 0:P], zeros[:, 0:2], start=False, stop=True, skip_group_check=True)
            ins.then_inc(A_done, 1)
            pe.wait_ge(hl_ready, T)
            for c in range(2):
                pe.wait_ge(A_copied, 2 * c + 2)
                for t in range(T):
                    ins = nc.tensor.transpose(wide(2 * c)[:, t, :], qk[:, t, P * c:P * (c + 1)], ident[0:TP, 0:TP])
                ins.then_inc(qkT_ps, 1)
            pe.wait_ge(pool_const, 2)
            pe.wait_ge(A_copied, T + 2)
            for hg in range(2):
                for t in range(T):
                    ins = mm(ps[:, 4 + hg, 0:P + 1], kx[:, t, hg, 0:P], kx[:, t, hg, :], start=(t == 0),
                             stop=(t == T - 1))
            ins.then_inc(m_ps, 1)
            for n in range(2 * H):
                h, w = n // 2, n % 2
                if n == 2:
                    pe.wait_ge(m_ready, 1)
                if n >= 4:
                    pe.wait_ge(st_copied_v if n % 2 else st_copied_a, (n - 4) // 2 + 1)
                for t in range(T):
                    parts = [(0, 0, 2 * D), (2 * D, D, 2 * D), (3 * D, 0, D)] if w else [(0, 0, 2 * D), (2 * D, 0, 2 * D)]
                    both = hl[:, t, w, h].rearrange("p i d -> p (i d)")
                    for at, lo, hi in parts:
                        ins = nc.tensor.transpose(wide_h(ST_BANKS[n % 4])[at:at + hi - lo, t, :], both[:, lo:hi],
                                                  identh[0:TP, 0:TP])
                ins.then_inc(st_ps, 1)
            pe.wait_ge(qkT_copied, 2)
            for hg in range(2):
                for lo, hi in SPLIT:
                    ins = mm(psf[:, 1024 * hg + lo:1024 * hg + hi], MA[:, hg, :], qT[:, hg, lo:hi],
                             start=True, stop=True)
                ins.then_inc(u_ps, 1)
            for hg in range(2):
                pe.wait_ge(u_ready, hg + 1)
                for lo, hi in SPLIT:
                    ins = mm(psf[:, 1024 * hg + lo:1024 * hg + hi], blk[:, :], uq[:, hg, lo:hi],
                             start=True, stop=True)
                ins.then_inc(n_ps, 1)
            pe.wait_ge(n_ready, 2)
            pe.wait_ge(st_copied_a, H)
            pe.wait_ge(st_copied_v, H)

            def scores(u):
                hg, hf, m, pr = units[u]
                lo, hi = HALF[hf]
                if u >= SLOTS:
                    pe.wait_ge(g_ready, u - SLOTS + 1)
                for i in range(2):
                    h = HG * hg + 2 * pr + i
                    ins = mm(ps[0:TP, 2 * (u % SLOTS) + i, 0:hi - lo], st[:, 1, h, TP * m:TP * (m + 1)],
                             st[:, 0, h, lo:hi], start=True, stop=True)
                ins.then_inc(s_ps, 1)

            def values(u2):
                hg, hf, m, _ = units[2 * u2]
                lo, hi = HALF[hf]
                k = 2 * hg + hf
                pe.wait_ge(g_ready, 2 * u2 + 2)
                if m == 0 and k >= 2:
                    pe.wait_ge(y_ready, k - 1)
                for pr in range(2):
                    for i in range(2):
                        h = 2 * pr + i
                        ins = mm(ps[D * h:D * (h + 1), 6 + k % 2, 0:hi - lo],
                                 v[:, m, P * hg + D * h:P * hg + D * (h + 1)],
                                 g[:, (2 * u2 + pr) % NGB, i, 0:hi - lo], start=(m == 0), stop=(m == T - 1),
                                 tile_position=(0, D * h), skip_group_check=True)
                ins.then_inc(g_used, 1)

            U2 = len(units) // 2
            scores(0)
            scores(1)
            for u2 in range(U2):
                if u2 + 1 < U2:
                    scores(2 * u2 + 2)
                    scores(2 * u2 + 3)
                values(u2)
            pe.wait_ge(g_ready, len(units))
            pe.wait_ge(y_ready, 4)
            for s in range(T):
                for t in range(T):
                    ins = nc.tensor.transpose(at_block(s, t), A[:, t, TP * s:TP * (s + 1)], ident[0:TP, 0:TP])
                ins.then_inc(AT_ps, 1)
            pe.wait_ge(in_wproj, 16)
            for t in range(T):
                if t >= 2:
                    pe.wait_ge(x2_ready, t - 1)
                own = slice(TP * t, TP * (t + 1))
                b, b2 = RP_BANKS[t % 2]
                for c in range(KC):
                    mm(ps[0:TP, b2, 0:C], xnT[:, c, own], wlr_sb[:, c, C:2 * C], start=(c == 0), stop=False)
                for c in range(KC):
                    mm(ps[0:TP, b2, 0:C], yT[:, c, own], wproj_sb[:, c, :], start=False, stop=(c == KC - 1))
                if t == 0:
                    pe.wait_ge(AT_copied, 7)
                for s in range(T):
                    ins = mm(ps[0:TP, b, 0:C + 1], AT[:, s, own], z[:, s, :], start=(s == 0), stop=(s == T - 1))
                ins.then_inc(rp_ps, 1)
            for t in range(T):
                pe.wait_ge(xn2_ready, t + 1)
                if t >= 4:
                    pe.wait_ge(x2T_ready, t - 3)
                for c in range(KC):
                    ins = nc.tensor.transpose(x2T_bank(t)[:, c], x2n[:, t, P * c:P * (c + 1)], ident[0:TP, 0:TP])
                ins.then_inc(x2T_ps, 1)

            def hidden(again):
                for k in range(KH):
                    if k >= 2:
                        pe.wait_ge(h_ready, again * KH + k - 1)
                    if not again and k == KH // 2 + 2:
                        gate(0)
                    if again and k == KH // 2:
                        pe.wait_ge(rows_back, 16)
                        for t in range(T):
                            ins = nc.tensor.transpose(wide(5)[0:E, t, :], selp[:, t, :], ident[0:TP, 0:TP])
                        ins.then_inc(selT_ps, 1)
                    for lo, hi in SPLIT:
                        for c in range(KC):
                            ins = mm(psf[:, 1024 * (k % 2) + lo:1024 * (k % 2) + hi],
                                     w1_sb[:, c, P * k:P * (k + 1)], x2nT[:, c, lo:hi],
                                     start=(c == 0), stop=(c == KC - 1))
                    ins.then_inc(f_ps, 1)

            def gate(half):
                pe.wait_ge(h_ready, 4 * (half + 1))
                for lo, hi in SPLIT:
                    for i in range(4):
                        k = 4 * half + i
                        ins = mm(psf[D * i:D * (i + 1), 4 * BANK + lo:4 * BANK + hi], wg_sb[:, k, :], hT[:, k, lo:hi],
                                 start=(half == 0), stop=(half == 1), tile_position=(0, D * i),
                                 skip_group_check=True)
                if half:
                    ins.then_inc(lgT_ps, 1)

            pe.wait_ge(in_w1, 16)
            pe.wait_ge(in_gate, 48)
            pe.wait_ge(x2T_ready, T)
            hidden(0)
            gate(1)
            pe.wait_ge(lgT_copied, 1)
            for t in range(T):
                ins = mm(ps[0:TP, 4, E * t:E * (t + 1)], lgT[:, TP * t:TP * (t + 1)], part_sum[:, :],
                         start=True, stop=True)
            ins.then_inc(lg_ps, 1)
            pe.wait_ge(rank_in, 1)
            sel = eq[:, :, :].rearrange("p t e -> p (t e)")
            mm(ps[0:TP, 5, 0:T * E], tri[:, :], sel, start=True, stop=True)
            mm(ps[0:TP, 6, 0:T * E], ones_c[0:TP, 0:TP], sel, start=True, stop=True).then_inc(rank_ps, 1)
            pe.wait_ge(xs_ready, 1)
            pe.wait_ge(perm_ready, T)
            for c in range(KC):
                for lo, hi in SPLIT:
                    for n in range(3 * T):
                        ins = mm(psf[:, 1024 * c + lo:1024 * c + hi], xs[:, n // T, n % T, P * c:P * (c + 1)],
                                 perm[:, n % T, lo:hi], start=(n == 0), stop=(n == 3 * T - 1))
                ins.then_inc(xT_ps, 1)
            pe.wait_ge(xT_ready, 2 * KC)
            hidden(1)
            pe.wait_ge(h_ready, 2 * KH)
            pe.wait_ge(selT_ready, 1)
            pe.wait_ge(in_bd, 16)
            for t in range(T):
                mm(ps[0:TP, t, 0:C], selT[:, TP * t:TP * (t + 1)], bd_sb[:, :],
                   start=True, stop=True).then_inc(bd_ps, 1)
            pe.wait_ge(in_wd, 16 * E)
            pe.wait_ge(stair_ready, 1)
            pe.sem_inc(e_ps, EB)
            with pe.Fori(0, STEPS // EB) as i:
                for b in range(EB):
                    e = pe.value_load(stair[0:1, 0, bass.ds(i * EB + b, 1)], max_val=E - 1)
                    pe.wait_ge(hT_staged, i * EB + (b + 1))
                    pe.wait_ge(acc_ready, i * EB + (T - EB + b + 1))
                    for k in range(KH):
                        ins = mm(ps[0:TP, b, 0:C], hT_step[:, b, k, :],
                                 wd_sb[:, bass.ds(e, 1), k, :], start=(k == 0), stop=(k == KH - 1))
                    ins.then_inc(e_ps, 1)


_OUT = (625, 256)


def kernel(**inputs):
    import numpy as np
    import concourse.bacc as bacc
    from concourse.bass_utils import run_bass_kernel_spmd

    a = {k: np.asarray(v) for k, v in inputs.items()}

    def rows(w, k):
        return np.ascontiguousarray(w.reshape(k, 128, -1).transpose(1, 0, 2))

    tp = 125
    arrays = {
        "x": np.ascontiguousarray(a["x"]),
        "src": np.ascontiguousarray(a["src"].reshape(-1, tp).T),
        "dst": np.ascontiguousarray(a["dst"].reshape(-1, tp).T),
        "w_qkv": rows(a["L0_mix_Wqkv"].T, 2),
        "b_qkv": a["L0_mix_bqkv"].reshape(1, -1),
        "w_lr": rows(np.concatenate([a["L0_gnn_W_l"].T, a["L0_gnn_W_r"].T], axis=1), 2),
        "b_r": a["L0_gnn_b_r"].reshape(1, -1),
        "w_proj": rows(a["L0_mix_Wproj"].T, 2),
        "b_proj": a["L0_mix_bproj"].reshape(1, -1),
        "temp": a["L0_mix_temperature"].reshape(1, -1),
        "w1": rows(a["L0_ffn_W1"], 2),
        "b1": np.ascontiguousarray(a["L0_ffn_b1"].reshape(8, 128).T),
        "wg": rows(a["L0_ffn_Wg"], 8),
        "bg": a["L0_ffn_bg"].reshape(1, -1),
        "wd": np.ascontiguousarray(a["L0_ffn_Wd"].reshape(8, 8, 128, 256).transpose(2, 0, 1, 3)),
        "bd": np.ascontiguousarray(a["L0_ffn_bd"]),
    }
    nc = bacc.Bacc("TRN2", target_bir_lowering=False, num_devices=1)
    args = [nc.dram_tensor(f"in_{n}", v.shape, mybir.dt.from_np(v.dtype), kind="ExternalInput").ap()
            for n, v in arrays.items()]
    out = nc.dram_tensor("out_0", _OUT, F32, kind="ExternalOutput").ap()
    rows_sorted = nc.dram_tensor("rows_sorted", (625, 521), F32, kind="Internal").ap()
    gps_layer(nc, *args, rows_sorted, out)
    r = run_bass_kernel_spmd(nc, [{f"in_{n}": v for n, v in arrays.items()}], core_ids=[0])
    return r.results[0]["out_0"]
```
